# Optimizing a Trainium2 kernel written in Bass

```python
import numpy as np
import jax
import jax.numpy as jnp

def _softmax(x, axis=-1):
    return jax.nn.softmax(x, axis=axis)

def _gelu(x):
    return jax.nn.gelu(x, approximate=True)

def _silu(x):
    return jax.nn.silu(x)

def _sigmoid(x):
    return jax.nn.sigmoid(x)

def _layernorm(x, axis=-1, eps=1e-05):
    m = jnp.mean(x, axis=axis, keepdims=True)
    v = jnp.var(x, axis=axis, keepdims=True)
    return (x - m) / jnp.sqrt(v + eps)

def _scatter_add(tgt, idx, src, axis=0):
    return tgt.at[idx].add(src)

def _segment_sum(src, seg, n):
    return jax.ops.segment_sum(src, seg, n)
kernel_name = 'mk_conv_seq_d4_conv_nchw32_r4_d70fd8'

def setup_inputs(seed: int=0):
    np.random.seed(seed)
    _w = jnp.asarray

    def _rec_inputs():
        import jax
        import jax.numpy as jnp
        _gk = jax.random.key(seed)
        x = -0.0002023 + 1 * jax.random.normal(jax.random.fold_in(_gk, 1), (16, 32, 28, 28), jnp.float32)
        return x
    x = _rec_inputs()

    def _L0_conv_setup():
        import jax, jax.numpy as jnp
        import numpy as np
        EPS = 1e-05
        DN = ('NCHW', 'OIHW', 'NCHW')

        def ternarize(w):
            aw = jnp.abs(w)
            delta = 0.7 * aw.mean()
            mask = (aw > delta).astype(w.dtype)
            alpha = (aw * mask).sum() / jnp.maximum(mask.sum(), 1.0)
            q = alpha * jnp.sign(w) * mask
            return w + jax.lax.stop_gradient(q - w)

        def bn(y, g, b, m, v):
            scale = (g / jnp.sqrt(v + EPS))[None, :, None, None]
            shift = (b - m * g / jnp.sqrt(v + EPS))[None, :, None, None]
            return y * scale + shift

        def relu6(y):
            return jnp.clip(y, 0.0, 6.0)

        def conv(x, w, stride=1, padding='VALID'):
            return jax.lax.conv_general_dilated(x, w, window_strides=(stride, stride), padding=padding, dimension_numbers=DN)
        key = jax.random.key(seed)
        ks = jax.random.split(key, 16)
        inp, oup, expand = (32, 32, 6)
        hidden = inp * expand
        B, H, W = (16, 28, 28)
        d = {}
        d['x'] = jax.random.normal(ks[0], (B, inp, H, W), dtype=jnp.float32)
        d['w1'] = jax.random.normal(ks[1], (hidden, inp, 1, 1), dtype=jnp.float32) * 0.1
        d['g1'] = 1.0 + 0.1 * jax.random.normal(ks[2], (hidden,), dtype=jnp.float32)
        d['b1'] = 0.1 * jax.random.normal(ks[3], (hidden,), dtype=jnp.float32)
        d['m1'] = 0.1 * jax.random.normal(ks[4], (hidden,), dtype=jnp.float32)
        d['v1'] = jax.random.uniform(ks[5], (hidden,), minval=0.5, maxval=1.5, dtype=jnp.float32)
        d['w2'] = jax.random.normal(ks[6], (hidden, hidden, 3, 3), dtype=jnp.float32) * 0.05
        d['g2'] = 1.0 + 0.1 * jax.random.normal(ks[7], (hidden,), dtype=jnp.float32)
        d['b2'] = 0.1 * jax.random.normal(ks[8], (hidden,), dtype=jnp.float32)
        d['m2'] = 0.1 * jax.random.normal(ks[9], (hidden,), dtype=jnp.float32)
        d['v2'] = jax.random.uniform(ks[10], (hidden,), minval=0.5, maxval=1.5, dtype=jnp.float32)
        d['w3'] = jax.random.normal(ks[11], (oup, hidden, 1, 1), dtype=jnp.float32) * 0.1
        d['g3'] = 1.0 + 0.1 * jax.random.normal(ks[12], (oup,), dtype=jnp.float32)
        d['b3'] = 0.1 * jax.random.normal(ks[13], (oup,), dtype=jnp.float32)
        d['m3'] = 0.1 * jax.random.normal(ks[14], (oup,), dtype=jnp.float32)
        d['v3'] = jax.random.uniform(ks[15], (oup,), minval=0.5, maxval=1.5, dtype=jnp.float32)
        return d
    _L0_conv_all = _L0_conv_setup()
    _L0_conv_in = {k: v for k, v in _L0_conv_all.items() if k in ('w1', 'g1', 'b1', 'm1', 'v1', 'w2', 'g2', 'b2', 'm2', 'v2', 'w3', 'g3', 'b3', 'm3', 'v3')}
    del _L0_conv_all

    def _L1_conv_setup():
        import jax, jax.numpy as jnp
        import numpy as np
        WBIT = 8
        XBIT = 8
        EPS = 1e-05

        def _ste(x, q):
            return x + jax.lax.stop_gradient(q - x)

        def fake_quant_weight(w, bits=WBIT):
            qmax = 2.0 ** (bits - 1) - 1.0
            s = jnp.maximum(jnp.max(jnp.abs(w)), 1e-08) / qmax
            q = jnp.clip(jnp.round(w / s), -qmax, qmax) * s
            return _ste(w, q)

        def fake_quant_act(x, bits=XBIT):
            qmax = 2.0 ** bits - 1.0
            s = jnp.maximum(jnp.max(x), 1e-08) / qmax
            q = jnp.clip(jnp.round(x / s), 0.0, qmax) * s
            return _ste(x, q)

        def asim_conv3x3(x, w, stride=1):
            xq = fake_quant_act(x)
            wq = fake_quant_weight(w)
            return jax.lax.conv_general_dilated(xq, wq, window_strides=(stride, stride), padding=((1, 1), (1, 1)), dimension_numbers=('NCHW', 'OIHW', 'NCHW'))

        def batchnorm(x, gamma, beta, mean, var):
            inv = jax.lax.rsqrt(var + EPS) * gamma
            return x * inv[None, :, None, None] + (beta - mean * inv)[None, :, None, None]
        key = jax.random.key(seed)
        ks = jax.random.split(key, 8)
        B, C, H, W = (32, 32, 40, 40)
        x = jax.random.uniform(ks[0], (B, C, H, W), dtype=jnp.float32)
        w1 = jax.random.normal(ks[1], (C, C, 3, 3), dtype=jnp.float32) * 0.05
        w2 = jax.random.normal(ks[2], (C, C, 3, 3), dtype=jnp.float32) * 0.05
        bn1_gamma = 1.0 + 0.1 * jax.random.normal(ks[3], (C,), dtype=jnp.float32)
        bn1_beta = 0.1 * jax.random.normal(ks[4], (C,), dtype=jnp.float32)
        bn1_mean = 0.1 * jax.random.normal(ks[5], (C,), dtype=jnp.float32)
        bn1_var = jax.random.uniform(ks[6], (C,), minval=0.5, maxval=1.5, dtype=jnp.float32)
        bn2_gamma = 1.0 + 0.1 * jax.random.normal(ks[7], (C,), dtype=jnp.float32)
        bn2_beta = jnp.zeros((C,), jnp.float32)
        bn2_mean = jnp.zeros((C,), jnp.float32)
        bn2_var = jnp.ones((C,), jnp.float32)
        return {'x': x, 'w1': w1, 'bn1_gamma': bn1_gamma, 'bn1_beta': bn1_beta, 'bn1_mean': bn1_mean, 'bn1_var': bn1_var, 'w2': w2, 'bn2_gamma': bn2_gamma, 'bn2_beta': bn2_beta, 'bn2_mean': bn2_mean, 'bn2_var': bn2_var}
    _L1_conv_all = _L1_conv_setup()
    _L1_conv_in = {k: v for k, v in _L1_conv_all.items() if k in ('w1', 'bn1_gamma', 'bn1_beta', 'bn1_mean', 'bn1_var', 'w2', 'bn2_gamma', 'bn2_beta', 'bn2_mean', 'bn2_var')}
    del _L1_conv_all

    def _L2_conv_setup():
        import jax, jax.numpy as jnp
        import numpy as np
        BN_EPS = 1e-05
        CUT_THRESH = 0.001
        key = jax.random.key(seed)
        k1, k2, k3 = jax.random.split(key, 3)
        B, Cin, Cout, H, W, K = (32, 32, 32, 48, 48, 3)
        return {'x': jax.random.normal(k1, (B, Cin, H, W), dtype=jnp.float32), 'conv_w': jax.random.normal(k2, (Cout, Cin, K, K), dtype=jnp.float32) * 0.05, 'conv_b': jax.random.normal(k3, (Cout,), dtype=jnp.float32) * 0.05, 'gamma': jnp.ones((Cout,), dtype=jnp.float32), 'beta': jnp.zeros((Cout,), dtype=jnp.float32), 'run_mean': jnp.zeros((Cout,), dtype=jnp.float32), 'run_var': jnp.ones((Cout,), dtype=jnp.float32)}
    _L2_conv_all = _L2_conv_setup()
    _L2_conv_in = {k: v for k, v in _L2_conv_all.items() if k in ('conv_w', 'conv_b', 'gamma', 'beta', 'run_mean', 'run_var')}
    del _L2_conv_all

    def _L3_conv_setup():
        import jax, jax.numpy as jnp
        import numpy as np
        BN_EPS = 1e-05
        CUT_THRESH = 0.001
        key = jax.random.key(seed)
        k1, k2, k3 = jax.random.split(key, 3)
        B, Cin, Cout, H, W, K = (32, 32, 32, 48, 48, 3)
        return {'x': jax.random.normal(k1, (B, Cin, H, W), dtype=jnp.float32), 'conv_w': jax.random.normal(k2, (Cout, Cin, K, K), dtype=jnp.float32) * 0.05, 'conv_b': jax.random.normal(k3, (Cout,), dtype=jnp.float32) * 0.05, 'gamma': jnp.ones((Cout,), dtype=jnp.float32), 'beta': jnp.zeros((Cout,), dtype=jnp.float32), 'run_mean': jnp.zeros((Cout,), dtype=jnp.float32), 'run_var': jnp.ones((Cout,), dtype=jnp.float32)}
    _L3_conv_all = _L3_conv_setup()
    _L3_conv_in = {k: v for k, v in _L3_conv_all.items() if k in ('conv_w', 'conv_b', 'gamma', 'beta', 'run_mean', 'run_var')}
    del _L3_conv_all
    return {'x': x, 'L0_conv_w1': _L0_conv_in['w1'], 'L0_conv_g1': _L0_conv_in['g1'], 'L0_conv_b1': _L0_conv_in['b1'], 'L0_conv_m1': _L0_conv_in['m1'], 'L0_conv_v1': _L0_conv_in['v1'], 'L0_conv_w2': _L0_conv_in['w2'], 'L0_conv_g2': _L0_conv_in['g2'], 'L0_conv_b2': _L0_conv_in['b2'], 'L0_conv_m2': _L0_conv_in['m2'], 'L0_conv_v2': _L0_conv_in['v2'], 'L0_conv_w3': _L0_conv_in['w3'], 'L0_conv_g3': _L0_conv_in['g3'], 'L0_conv_b3': _L0_conv_in['b3'], 'L0_conv_m3': _L0_conv_in['m3'], 'L0_conv_v3': _L0_conv_in['v3'], 'L1_conv_w1': _L1_conv_in['w1'], 'L1_conv_bn1_gamma': _L1_conv_in['bn1_gamma'], 'L1_conv_bn1_beta': _L1_conv_in['bn1_beta'], 'L1_conv_bn1_mean': _L1_conv_in['bn1_mean'], 'L1_conv_bn1_var': _L1_conv_in['bn1_var'], 'L1_conv_w2': _L1_conv_in['w2'], 'L1_conv_bn2_gamma': _L1_conv_in['bn2_gamma'], 'L1_conv_bn2_beta': _L1_conv_in['bn2_beta'], 'L1_conv_bn2_mean': _L1_conv_in['bn2_mean'], 'L1_conv_bn2_var': _L1_conv_in['bn2_var'], 'L2_conv_conv_w': _L2_conv_in['conv_w'], 'L2_conv_conv_b': _L2_conv_in['conv_b'], 'L2_conv_gamma': _L2_conv_in['gamma'], 'L2_conv_beta': _L2_conv_in['beta'], 'L2_conv_run_mean': _L2_conv_in['run_mean'], 'L2_conv_run_var': _L2_conv_in['run_var'], 'L3_conv_conv_w': _L3_conv_in['conv_w'], 'L3_conv_conv_b': _L3_conv_in['conv_b'], 'L3_conv_gamma': _L3_conv_in['gamma'], 'L3_conv_beta': _L3_conv_in['beta'], 'L3_conv_run_mean': _L3_conv_in['run_mean'], 'L3_conv_run_var': _L3_conv_in['run_var']}

def reference(x, L0_conv_w1, L0_conv_g1, L0_conv_b1, L0_conv_m1, L0_conv_v1, L0_conv_w2, L0_conv_g2, L0_conv_b2, L0_conv_m2, L0_conv_v2, L0_conv_w3, L0_conv_g3, L0_conv_b3, L0_conv_m3, L0_conv_v3, L1_conv_w1, L1_conv_bn1_gamma, L1_conv_bn1_beta, L1_conv_bn1_mean, L1_conv_bn1_var, L1_conv_w2, L1_conv_bn2_gamma, L1_conv_bn2_beta, L1_conv_bn2_mean, L1_conv_bn2_var, L2_conv_conv_w, L2_conv_conv_b, L2_conv_gamma, L2_conv_beta, L2_conv_run_mean, L2_conv_run_var, L3_conv_conv_w, L3_conv_conv_b, L3_conv_gamma, L3_conv_beta, L3_conv_run_mean, L3_conv_run_var):
    import jax
    import jax.numpy as jnp

    def _L0_conv_ref(x, w1, g1, b1, m1, v1, w2, g2, b2, m2, v2, w3, g3, b3, m3, v3):
        import jax, jax.numpy as jnp
        import numpy as np
        EPS = 1e-05
        DN = ('NCHW', 'OIHW', 'NCHW')

        def ternarize(w):
            aw = jnp.abs(w)
            delta = 0.7 * aw.mean()
            mask = (aw > delta).astype(w.dtype)
            alpha = (aw * mask).sum() / jnp.maximum(mask.sum(), 1.0)
            q = alpha * jnp.sign(w) * mask
            return w + jax.lax.stop_gradient(q - w)

        def bn(y, g, b, m, v):
            scale = (g / jnp.sqrt(v + EPS))[None, :, None, None]
            shift = (b - m * g / jnp.sqrt(v + EPS))[None, :, None, None]
            return y * scale + shift

        def relu6(y):
            return jnp.clip(y, 0.0, 6.0)

        def conv(x, w, stride=1, padding='VALID'):
            return jax.lax.conv_general_dilated(x, w, window_strides=(stride, stride), padding=padding, dimension_numbers=DN)
        h = relu6(bn(conv(x, ternarize(w1)), g1, b1, m1, v1))
        h = relu6(bn(conv(h, ternarize(w2), stride=1, padding=((1, 1), (1, 1))), g2, b2, m2, v2))
        h = bn(conv(h, ternarize(w3)), g3, b3, m3, v3)
        return x + h

    def _L1_conv_ref(x, w1, bn1_gamma, bn1_beta, bn1_mean, bn1_var, w2, bn2_gamma, bn2_beta, bn2_mean, bn2_var):
        import jax, jax.numpy as jnp
        import numpy as np
        WBIT = 8
        XBIT = 8
        EPS = 1e-05

        def _ste(x, q):
            return x + jax.lax.stop_gradient(q - x)

        def fake_quant_weight(w, bits=WBIT):
            qmax = 2.0 ** (bits - 1) - 1.0
            s = jnp.maximum(jnp.max(jnp.abs(w)), 1e-08) / qmax
            q = jnp.clip(jnp.round(w / s), -qmax, qmax) * s
            return _ste(w, q)

        def fake_quant_act(x, bits=XBIT):
            qmax = 2.0 ** bits - 1.0
            s = jnp.maximum(jnp.max(x), 1e-08) / qmax
            q = jnp.clip(jnp.round(x / s), 0.0, qmax) * s
            return _ste(x, q)

        def asim_conv3x3(x, w, stride=1):
            xq = fake_quant_act(x)
            wq = fake_quant_weight(w)
            return jax.lax.conv_general_dilated(xq, wq, window_strides=(stride, stride), padding=((1, 1), (1, 1)), dimension_numbers=('NCHW', 'OIHW', 'NCHW'))

        def batchnorm(x, gamma, beta, mean, var):
            inv = jax.lax.rsqrt(var + EPS) * gamma
            return x * inv[None, :, None, None] + (beta - mean * inv)[None, :, None, None]
        identity = x
        out = asim_conv3x3(x, w1, stride=1)
        out = batchnorm(out, bn1_gamma, bn1_beta, bn1_mean, bn1_var)
        out = jax.nn.relu(out)
        out = asim_conv3x3(out, w2, stride=1)
        out = batchnorm(out, bn2_gamma, bn2_beta, bn2_mean, bn2_var)
        out = out + identity
        return jax.nn.relu(out)

    def _L2_conv_ref(x, conv_w, conv_b, gamma, beta, run_mean, run_var):
        import jax, jax.numpy as jnp
        import numpy as np
        BN_EPS = 1e-05
        CUT_THRESH = 0.001
        y = jax.lax.conv_general_dilated(x, conv_w, window_strides=(1, 1), padding=((1, 1), (1, 1)), dimension_numbers=('NCHW', 'OIHW', 'NCHW'))
        y = y + conv_b[None, :, None, None]
        inv_std = gamma * jax.lax.rsqrt(run_var + BN_EPS)
        y = (y - run_mean[None, :, None, None]) * inv_std[None, :, None, None] + beta[None, :, None, None]
        y = jnp.maximum(y, 0.0)
        chan_absmax = jnp.max(jnp.abs(y), axis=(2, 3), keepdims=True)
        return jnp.where(chan_absmax < CUT_THRESH, jnp.zeros_like(y), y)

    def _L3_conv_ref(x, conv_w, conv_b, gamma, beta, run_mean, run_var):
        import jax, jax.numpy as jnp
        import numpy as np
        BN_EPS = 1e-05
        CUT_THRESH = 0.001
        y = jax.lax.conv_general_dilated(x, conv_w, window_strides=(1, 1), padding=((1, 1), (1, 1)), dimension_numbers=('NCHW', 'OIHW', 'NCHW'))
        y = y + conv_b[None, :, None, None]
        inv_std = gamma * jax.lax.rsqrt(run_var + BN_EPS)
        y = (y - run_mean[None, :, None, None]) * inv_std[None, :, None, None] + beta[None, :, None, None]
        y = jnp.maximum(y, 0.0)
        chan_absmax = jnp.max(jnp.abs(y), axis=(2, 3), keepdims=True)
        return jnp.where(chan_absmax < CUT_THRESH, jnp.zeros_like(y), y)

    def _gn(v, G=16, eps=1e-05):
        B_, C_, H_, W_ = v.shape
        g = v.reshape(B_, G, C_ // G, H_, W_)
        m = jnp.mean(g, axis=(2, 3, 4), keepdims=True)
        s = jnp.var(g, axis=(2, 3, 4), keepdims=True)
        return ((g - m) / jnp.sqrt(s + eps)).reshape(v.shape)

    def _ln_c(v, eps=1e-06):
        m = jnp.mean(v, axis=1, keepdims=True)
        s = jnp.var(v, axis=1, keepdims=True)
        return (v - m) / jnp.sqrt(s + eps)

    def _ln_t(v, eps=1e-05):
        m = jnp.mean(v, axis=-1, keepdims=True)
        s = jnp.var(v, axis=-1, keepdims=True)
        return (v - m) / jnp.sqrt(s + eps)

    def _to_tokens(v):
        B_, C_, H_, W_ = v.shape
        return v.reshape(B_, C_, H_ * W_).transpose(0, 2, 1)

    def _from_tokens(t, like):
        B_, C_, H_, W_ = like.shape
        return t.transpose(0, 2, 1).reshape(B_, C_, H_, W_)
    x = _L0_conv_ref(x, L0_conv_w1, L0_conv_g1, L0_conv_b1, L0_conv_m1, L0_conv_v1, L0_conv_w2, L0_conv_g2, L0_conv_b2, L0_conv_m2, L0_conv_v2, L0_conv_w3, L0_conv_g3, L0_conv_b3, L0_conv_m3, L0_conv_v3)
    x = _L1_conv_ref(x, L1_conv_w1, L1_conv_bn1_gamma, L1_conv_bn1_beta, L1_conv_bn1_mean, L1_conv_bn1_var, L1_conv_w2, L1_conv_bn2_gamma, L1_conv_bn2_beta, L1_conv_bn2_mean, L1_conv_bn2_var)
    x = _L2_conv_ref(x, L2_conv_conv_w, L2_conv_conv_b, L2_conv_gamma, L2_conv_beta, L2_conv_run_mean, L2_conv_run_var)
    x = _L3_conv_ref(x, L3_conv_conv_w, L3_conv_conv_b, L3_conv_gamma, L3_conv_beta, L3_conv_run_mean, L3_conv_run_var)
    return x

_drawn_inputs = setup_inputs


def setup_inputs(seed=0):
    import zlib

    import numpy as np

    out = dict(_drawn_inputs(seed))
    spreads = {'L1_conv_bn2_beta': (0.0, 0.1),
     'L1_conv_bn2_mean': (0.0, 0.1),
     'L1_conv_bn2_var': (1.0, 0.2),
     'L2_conv_gamma': (1.0, 0.2),
     'L2_conv_beta': (0.0, 0.1),
     'L2_conv_run_mean': (0.0, 0.1),
     'L2_conv_run_var': (1.0, 0.2),
     'L3_conv_gamma': (1.0, 0.2),
     'L3_conv_beta': (0.0, 0.1),
     'L3_conv_run_mean': (0.0, 0.1),
     'L3_conv_run_var': (1.0, 0.2)}
    factors = {}
    for name, (base, spread) in spreads.items():
        noise = np.random.default_rng([zlib.crc32(name.encode()), seed]).standard_normal(out[name].shape)
        drawn = base * np.exp(spread * noise) if base else spread * noise
        out[name] = jnp.asarray(drawn.astype(out[name].dtype))
    for name, factor in factors.items():
        out[name] = (out[name] * factor).astype(out[name].dtype)
    return out
```

```python
from contextlib import ExitStack

import concourse.bass as bass
from concourse import mybir

P = 128
B, C, H, W = 16, 32, 28, 28
HID = 192
G = P // C
NCH = B // G
HW = H * W
HALF_ROWS = H // 2
HALF = HALF_ROWS * W
PW = W + 2
PAD = (H + 2) * PW
TAPS = 9
TR = H // 2
HB = HID - P
EPS = 1e-5
CUT = 1e-3
S0 = 4096.0
CAP = 6.0 * S0
MAGIC = 1.5 * 2.0 ** 23
XQ = 255.0
WQ = 127.0
F16_TOP = 2.0 ** 14

F32 = mybir.dt.float32
F16 = mybir.dt.float16
BF16 = mybir.dt.bfloat16
I32 = mybir.dt.int32
ALU = mybir.AluOpType
ACT = mybir.ActivationFunctionType
AX = mybir.AxisListType

BN1A, BN1B, BN2A, BN2B, BN3, BNQ1, BNQ2, BNC, BND = range(9)
NBN = 9
KG, KB, KM, KV = range(4)
NPAR = 4 * NBN + 2

TAIL = [("q", 0), ("q", 1), ("q", 2), ("c", 0), ("q", 3), ("c", 1), ("d", 0), ("c", 2), ("d", 1),
        ("c", 3), ("d", 2), ("d", 3)]
A_SHARE = [(0, 0), (1, 0)]
V_SHARE = [(g, k) for k in range(2) for g in range(G) if (g, k) not in A_SHARE]
XK = [16 * 3 * (G - 2)] + [16 * 3 * G] * (NCH - 1)
TOTAL_BANK = {1: 4, 2: 5, 3: 7, 4: 7}
QBANK = (0, 6)
LTAIL = [s for s in TAIL if s[0] != "q"]
DONE_BEFORE = {(k, c): (LTAIL.index((k, c - 1)) + 1 if c else 0) for k, c in LTAIL}

N1, N2, N3 = C * HID, HID * HID * TAPS, HID * C


def conv_seq(nc, x, params, w1, w2a, w2b, w3, wq1, wq2, wc, wd, out):
    with ExitStack() as ctx:
        def sb(name, shape, dt):
            return ctx.enter_context(nc.sbuf_tensor(name, shape, dt))

        def sem(name):
            return ctx.enter_context(nc.semaphore(name))

        par = sb("par", [P, NPAR], F32)
        xin = sb("xin", [P, NCH, HW], F32)
        w1r = sb("w1r", [C, HID], F32)
        big = sb("big", [P, 5, TAPS * HID], F32)
        w2ar, w2br, wjunk, ajunk = (big[:, k, :] for k in range(4))
        wneg = big[:, 4, :].bitcast(F16)[:, 0:TAPS * HID]
        kst = big[:].rearrange("p k f -> p (k f)").bitcast(F16)[:, 0:4 * G * PAD].rearrange(
            "p (l b g h w) -> p l b g h w", l=2, b=2, g=G, h=H + 2)
        w3r = sb("w3r", [P, 2, C], F32)
        wqr = sb("wqr", [P, 2, TAPS * C], F32)
        wcr = sb("wcr", [P, 2, TAPS * C], F32)
        w1t = sb("w1t", [96, HID + HB], BF16)
        w2at = sb("w2at", [P, TAPS, HID], F16)
        w2bt = sb("w2bt", [P, TAPS, HID], F16)
        w3t = sb("w3t", [P, 2, C], F16)
        xpart = sb("xpart", [P, 2, 3, HW], BF16)
        xrest = sb("xrest", [P, 2, HW], F32)
        xk = sb("xk", [96, B, HW], BF16)
        ra = sb("ra", [P, 2, HW], F32)
        hp = sb("hp", [P, H + 2, PW], F32)
        va = sb("va", [P, 4, TR, PW], F32)
        vh = sb("vh", [P, 2, 2, 4, TR, PW], F16)
        hb = sb("hb", [P, 2, H + 2, PW], F16)
        wu = sb("wu", [P, 2, 3, HID], F16)
        wun = sb("wun", [P, 3, HB], F16)
        c1a = sb("c1a", [P, HALF], F32)
        ds = sb("ds", [P, 2, HALF], F32)
        cy = sb("cy", [P, HALF], F32)
        r2a = sb("r2a", [P, HW], F32)
        r2b = sb("r2b", [P, HALF], F32)
        h2a = sb("h2a", [P, G, 2, HW], F16)
        h2b = sb("h2b", [P, G, 2, HALF], F16)
        y0 = sb("y0", [P, NCH, HW], F32)
        col = sb("col", [P, 64], F32)
        bn = sb("bn", [P, 8, NBN], F32)
        mx = sb("mx", [P, 16], F32)
        expo = sb("expo", [P, NBN], F32)
        ident = sb("ident", [P, P], F32)
        ones = sb("ones", [P, P], F32)
        rowm = sb("rowm", [P, 4], F32)
        diag = sb("diag", [P, 8], F32)
        mxa = sb("mxa", [P, 8], F32)
        wqq = sb("wqq", [P, 2, TAPS * C], F32)
        wqi = sb("wqi", [P, 2, TAPS, P], BF16)
        wst = sb("wst", [P, 2, TAPS * C], F16)
        qf = ra
        qi = sb("qi", [P, NCH, H + 2, PW], BF16)
        h1 = h2a[:].rearrange("p g k f -> p g (k f)").bitcast(F32)
        t1 = va[:].rearrange("p k h w -> p (k h w)")[:, 0:2 * HW].rearrange("p (b f) -> p b f", b=2)
        yb = vh[:].rearrange("p b s k h w -> p (b s k h w)").bitcast(F32)[:, 0:2 * HW].rearrange(
            "p (b f) -> p b f", b=2)
        part = sb("part", [P, 2, 2, 2, H + 2, PW], F16)
        raj = [ra[:], part[:, 1].rearrange("p b k h w -> p (b k h w)").bitcast(F32)[:, 0:2 * HW].rearrange(
            "p (b f) -> p b f", b=2)]
        om = xin
        cm = sb("cm", [P, 2, NCH, 2], F32)

        ps = ctx.enter_context(nc.psum_tensor("ps", [P, 8, 512], F32))

        s_par, s_w1, s_w2b, s_w3, s_wq, s_wc = map(sem, ("s_par", "s_w1", "s_w2b", "s_w3", "s_wq", "s_wc"))
        s_w2a = [sem(f"s_w2a{k}") for k in range(3)]
        s_x = [sem(f"s_x{c}") for c in range(NCH)]
        s_ximg1 = sem("s_ximg1")
        s_xk = [sem(f"s_xk{c}") for c in range(NCH)]
        s_dup = [[sem(f"s_dup{l}_{k}") for k in range(NCH)] for l in range(2)]
        s_out = sem("s_out")
        pool_zeroed, pool_ident, x_split, pool_chain = map(
            sem, ("pool_zeroed", "pool_ident", "x_split", "pool_chain"))
        v_chain, a_chain, sums_ready, sums_done, w1_ready, w2_ready, w3_ready = map(
            sem, ("v_chain", "a_chain", "sums_ready", "sums_done", "w1_ready", "w2_ready", "w3_ready"))
        a_sum, inv_ready, thr_ready, bn1_ready, bn_ready, mxt_go, mxt_done, wl_ready = map(
            sem, ("a_sum", "inv_ready", "thr_ready", "bn1_ready", "bn_ready", "mxt_go", "mxt_done", "wl_ready"))
        expa_done, expb_done, m_done, convb_done, proj_done = map(
            sem, ("expa_done", "expb_done", "m_done", "convb_done", "proj_done"))
        ra_ready, rb_ready, vhi_ready, c1_ready, cy_ready, r2a_ready, r2b_ready, xs_ready, x0_ready = map(
            sem, ("ra_ready", "rb_ready", "vhi_ready", "c1_ready", "cy_ready", "r2a_ready", "r2b_ready",
                  "xs_ready", "x0_ready"))
        hp_done, v_ready, va_ready, hbhi_done, hb_ready, out_v, z_half, z_ready = map(
            sem, ("hp_done", "v_ready", "va_ready", "hbhi_done", "hb_ready", "out_v", "z_half", "z_ready"))
        h2hi_done, h2a_ready, h2_ready, y0_ready = map(
            sem, ("h2hi_done", "h2a_ready", "h2_ready", "y0_ready"))
        gm_go, gm_done, q_v, q_ready, q1_done, h1_ready, q2_done, t1_ready, ys_ready = map(
            sem, ("gm_go", "gm_done", "q_v", "q_ready", "q1_done", "h1_ready", "q2_done", "t1_ready", "ys_ready"))
        scale_ready = sem("scale_ready")
        a_abs = sem("a_abs")
        w3s_ready = sem("w3s_ready")
        wst_ready = sem("wst_ready")
        part_ready = [sem(f"part_ready{l}") for l in range(2)]
        stack_v = [sem(f"stack_v{l}") for l in range(2)]
        stack_a = [sem(f"stack_a{l}") for l in range(2)]
        lconv_done = [sem(f"lconv_done{l}") for l in range(2)]
        yb_ready = sem("yb_ready")
        o_ready = sem("o_ready")
        cmax_done = sem("cmax_done")

        block = ctx.enter_context(nc.Block())

        def wait(eng, s, n):
            if not (isinstance(n, int) and n <= 0):
                eng.wait_ge(s, n)

        def inner(t, r0=0, rows=H):
            return t[:, 1 + r0:1 + r0 + rows, 1:1 + W]

        def by_rows(t, odd):
            return t.rearrange("p (t k w) -> p t k w", t=TR, k=2)[:, :, odd, :]

        def img(t, rows=H):
            return t.rearrange("p (h w) -> p h w", h=rows)

        SUMS, NSUM = 0, 3
        SB = 3
        TOT = 6
        DEL, NDEL = 9, 12
        PART1, PART2 = 15, 21
        AL = 27
        TMP = 30
        TOT2 = 33
        GMX, GSC = 40, 41
        SIG = 44
        BSC, BSH = 0, 1
        BT = 2
        MW1, MW2, MC, MD, MI2, MH2, MIC, MHC = range(8)

        @block.sync
        def _(sp):
            sp.dma_start(xin[:, 0, :], x[:, 0, :]).then_inc(s_x[0], 16)
            for k in range(3):
                dy = slice(3 * HID * k, 3 * HID * k + 3 * HID)
                sp.dma_start(w2ar[:, dy], w2a[:, dy]).then_inc(s_w2a[k], 16)
            for c in range(1, NCH):
                sp.dma_start(xin[:, c, :], x[:, c, :]).then_inc(s_x[c], 16)
            sp.dma_start(w3r[:, 0, :], w3[0:P]).then_inc(s_w3, 16)
            sp.dma_start(w3r[0:HB, 1, :], w3[P:HID]).then_inc(s_w3, 16)
            sp.dma_start(w3r[HB:P, 1, :], w3[P:HID]).then_inc(s_w3, 16)

            def spread(c):
                sp.wait_ge(x_split, c + 1)
                for g in range(0 if c else 1, G):
                    for k in range(3):
                        sp.dma_start(xk[C * k:C * k + C, G * c + g, :],
                                     xpart[C * g:C * g + C, c % 2, k, :]).then_inc(s_ximg1 if (c, g) == (0, 1) else s_xk[c], 16)

            spread(0)
            for g in range(G):
                q = slice(C * g, C * g + C)
                for k, w in enumerate((wq1, wq2)):
                    sp.dma_start(wqr[q, k, :], w).then_inc(s_wq, 16)
                for k, w in enumerate((wc, wd)):
                    sp.dma_start(wcr[q, k, :], w).then_inc(s_wc, 16)
            for c in range(1, NCH):
                spread(c)

            def dup(layer, c):
                sp.wait_ge(stack_v[layer], c + 1)
                sp.wait_ge(stack_a[layer], c + 1)
                sp.dma_start(kst[2 * C:P, layer, c % 2].rearrange("p g h w -> p (g h w)"),
                             kst[0:2 * C, layer, c % 2].rearrange("p g h w -> p (g h w)")).then_inc(s_dup[layer][c], 16)

            for kind, c in TAIL:
                if kind == "q":
                    dup(0, c)
                elif kind == "c":
                    dup(1, c)
                else:
                    sp.wait_ge(o_ready, c + 1)
                    sp.dma_start(out[:, c, :], om[:, c, :]).then_inc(s_out, 16)
            sp.wait_ge(s_out, 16 * NCH)

        @block.gpsimd
        def _(pool):
            nc.gpsimd.memset(col[:], 0.0).then_inc(pool_zeroed, 1)
            nc.gpsimd.memset(ones[:], 1.0).then_inc(pool_zeroed, 1)

            n = [0]

            def link(ins):
                n[0] += 1
                ins.then_inc(pool_chain, 1)
                pool.wait_ge(pool_chain, n[0])

            def split(c):
                pool.wait_ge(s_x[c], 16)
                if c >= 2:
                    pool.wait_ge(s_ximg1, 48)
                    pool.wait_ge(s_xk[c - 2], XK[c - 2])
                b = [xpart[:, c % 2, k, :] for k in range(3)]
                r = [xrest[:, 0, :], xrest[:, 1, :]]
                link(nc.gpsimd.tensor_copy(b[0], xin[:, c, :]))
                link(nc.gpsimd.tensor_tensor(r[0], xin[:, c, :], b[0], ALU.subtract))
                link(nc.gpsimd.tensor_copy(b[1], r[0]))
                link(nc.gpsimd.tensor_tensor(r[1], r[0], b[1], ALU.subtract))
                nc.gpsimd.tensor_copy(b[2], r[1]).then_inc(x_split, 1)

            nc.gpsimd.memset(expo[:], -0.5).then_inc(pool_zeroed, 1)
            nc.gpsimd.memset(hp[:], 0.0).then_inc(pool_zeroed, 1)

            pool.wait_ge(s_par, 16)
            pool.wait_ge(pool_zeroed, 3)
            kind = [par[:, NBN * k:NBN * k + NBN] for k in range(4)]
            link(nc.gpsimd.tensor_scalar(bn[:, BT, :], kind[KV], EPS, None, ALU.add))
            link(nc.gpsimd.tensor_tensor(bn[:, BT + 1, :], bn[:, BT, :], expo[:], ALU.pow))
            link(nc.gpsimd.tensor_tensor(bn[:, BSC, :], bn[:, BT + 1, :], kind[KG], ALU.mult))
            link(nc.gpsimd.tensor_tensor(kind[KM][:, BNC:BND + 1], kind[KM][:, BNC:BND + 1],
                                         par[:, 4 * NBN:4 * NBN + 2], ALU.subtract))
            link(nc.gpsimd.tensor_tensor(bn[:, BT, :], kind[KM], bn[:, BSC, :], ALU.mult))
            link(nc.gpsimd.tensor_tensor(bn[:, BSH, :], kind[KB], bn[:, BT, :], ALU.subtract))
            nc.gpsimd.tensor_scalar(bn[:, BSH, BN1A:BN3], bn[:, BSH, BN1A:BN3], S0, None, ALU.mult).then_inc(inv_ready, 1)
            for b in range(2):
                nc.gpsimd.memset(hb[:, b], 0.0).then_inc(pool_zeroed, 1)
            link(nc.gpsimd.memset(ident[:], 0.0))
            nc.gpsimd.affine_select(out=ident[:], in_=ident[:], compare_op=ALU.not_equal, fill=1.0, base=0,
                                    pattern=[[-1, P]], channel_multiplier=1).then_inc(pool_ident, 1)
            pool.wait_ge(x0_ready, 1)
            for c in range(1, NCH):
                split(c)
            nc.gpsimd.memset(qi[:], 0.0).then_inc(pool_zeroed, 1)
            nc.gpsimd.memset(wqi[:], 0.0).then_inc(pool_zeroed, 1)
            nc.gpsimd.memset(part[:, 0], 0.0).then_inc(pool_zeroed, 1)
            pool.wait_ge(hb_ready, B)
            nc.gpsimd.memset(part[:, 1], 0.0).then_inc(pool_zeroed, 1)

        @block.tensor
        def _(pe):
            pe.wait_ge(pool_zeroed, 2)
            def total(n, w, *cols):
                for k, c in enumerate(cols):
                    i = nc.tensor.matmul(ps[:, TOTAL_BANK[n], 8 * n:8 * n + w], ones[:], c, start=(k == 0),
                                         stop=(k == len(cols) - 1))
                i.then_inc(sums_done, 1)

            pe.wait_ge(sums_ready, 1)
            total(1, 1, col[:, SUMS:SUMS + 1])

            def expand(j, n, bank=6):
                two, h = divmod(n, 2)
                if n == 0:
                    if isinstance(j, int) and j == 1:
                        pe.wait_ge(s_ximg1, 48)
                    if isinstance(j, int) and j in (2, G):
                        pe.wait_ge(s_xk[j // G], XK[j // G])
                    wait(pe, rb_ready, 2 * j)
                elif bank == 6:
                    pe.wait_ge(*((ra_ready, 2 * j + n) if n < 3 else (rb_ready, 2 * j + 1)))
                nc.tensor.matmul(ps[:, bank, :HALF], (w1t[:, 0:P], w1t[:, P:P + 2 * HB])[two],
                                 xk[:, j, HALF * h:HALF * h + HALF],
                                 start=True, stop=True).then_inc((expa_done, expb_done)[two], 1)

            def weights(k, dx, rest):
                o = slice(P, HID) if rest else slice(0, P)
                if k in (0, 3):
                    return w2at[:, 2 * k + dx, o]
                return wun[:, dx, :] if rest and k == 2 else wu[:, k - 1, dx, o]

            def rows(b, odd, t):
                dy, dx = divmod(t, 3)
                r0 = dy + odd
                return hb[:, b, r0:r0 + 2 * TR - 1:2, dx:dx + W]

            def product(k, b, wino=True, plain=True):
                last = k in (1, 2)
                if wino:
                    for part in range(2):
                        for dx in range(3):
                            i = nc.tensor.matmul(ps[:, k, :HALF], weights(k, dx, False),
                                                 vh[:, b, part, k, :, dx:dx + W], start=(part == 0 and dx == 0),
                                                 stop=(last and part == 1 and dx == 2))
                if plain and not last:
                    for t in range(TAPS):
                        i = nc.tensor.matmul(ps[:, k, :HALF], w2bt[:, t, 0:P], rows(b, k // 3, t), start=False,
                                             stop=(t == TAPS - 1))
                if last or plain:
                    i.then_inc(m_done, 1)

            def pair(bank, ks, b):
                plain = bank == 5
                for part in range(2):
                    for dx in range(3):
                        for q, k in enumerate(ks):
                            i = nc.tensor.matmul(ps[HB * q:HB * q + HB, bank, :HALF], weights(k, dx, True),
                                                 vh[:, b, part, k, :, dx:dx + W], start=(part == 0 and dx == 0),
                                                 stop=(not plain and part == 1 and dx == 2))
                if plain:
                    for t in range(TAPS):
                        for q in range(2):
                            i = nc.tensor.matmul(ps[HB * q:HB * q + HB, bank, :HALF], w2bt[:, t, P:HID],
                                                 rows(b, q, t), start=False, stop=(t == TAPS - 1))
                    i.then_inc(convb_done, 1)

            def project(c, h, steps=(0, 1, 2, 3), bank=7):
                wait(pe, y0_ready, 2 * c + h if bank == 7 else 0)
                lower = slice(HB * h, HB * h + HB)
                for s in steps:
                    if s < 2:
                        pe.wait_ge((h2a_ready, h2_ready)[s], (c + 1) * G)
                    for g in range(G):
                        w, rhs = ((w3t[:, 0, :], by_rows(h2a[:, g, s, :], h)) if s < 2 else
                                  (w3t[lower, 1, :], h2b[lower, g, s - 2, :]))
                        i = nc.tensor.matmul(ps[C * g:C * g + C, bank, :HALF], w, rhs, start=(s == 0), stop=(s == 3))
                if 3 in steps:
                    i.then_inc(proj_done, 1)

            def slot(c, g, first=False, last=False):
                j = c * G + g
                b = g % 2
                ahead = not last or g < G - 2
                if first and g == 0:
                    pe.wait_ge(w2_ready, 1)
                    pe.wait_ge(va_ready, 1)
                    product(0, b, plain=False)
                    product(3, b, plain=False)
                    expand(j + 2, 0)
                    pe.wait_ge(w2_ready, 2)
                    product(1, b)
                    product(2, b)
                    expand(j + 2, 1)
                    pe.wait_ge(w2_ready, 3)
                    pe.wait_ge(hb_ready, 1)
                    product(0, b, wino=False)
                    expand(j + 2, 2)
                    product(3, b, wino=False)
                    expand(j + 2, 3)
                    pe.wait_ge(sums_ready, 3)
                    pe.wait_ge(a_sum, 4)
                    total(4, 6, col[:, PART1:PART1 + 6], col[:, PART2:PART2 + 6])
                else:
                    if ahead:
                        expand(j + 2, 0)
                    pe.wait_ge(va_ready, j + 1)
                    pe.wait_ge(c1_ready, j)
                    product(1, b)
                    pe.wait_ge(out_v, 3 * j - 2)
                    product(2, b)
                    if ahead:
                        expand(j + 2, 1)
                    pe.wait_ge(out_v, 3 * j - 1)
                    pe.wait_ge(hb_ready, j + 1)
                    product(0, b)
                    if ahead:
                        expand(j + 2, 2)
                    if g == 0 and not first:
                        if isinstance(c, int) is False:
                            pe.wait_ge(w3_ready, 1)
                        project(c - 1, 0)
                    pe.wait_ge(out_v, 3 * j)
                    product(3, b)
                    if ahead:
                        expand(j + 2, 3)
                    pe.wait_ge(z_ready, j)
                pair(4, (1, 2), b)
                if g == 0 and not first:
                    project(c - 1, 1)
                pair(5, (0, 3), b)

            pe.wait_ge(w1_ready, 1)
            pe.wait_ge(x0_ready, 1)
            for n in range(4):
                expand(0, n, bank=n)
            pe.wait_ge(sums_ready, 2)
            total(2, 2, col[:, PART1:PART1 + 4:3])
            pe.wait_ge(w3s_ready, 1)
            pe.wait_ge(a_sum, 1)
            total(3, 2, col[:, SUMS + 1:SUMS + 3], col[:, SB + 1:SB + 3])
            for n in range(4):
                expand(1, n)
            slot(0, 0, first=True)
            slot(0, 1, first=True)
            pe.wait_ge(pool_ident, 1)
            pe.wait_ge(mxt_go, 1)
            nc.tensor.transpose(ps[0:8, 7, P:2 * P], mx[:, 0:8], ident[:]).then_inc(mxt_done, 1)
            slot(0, 2, first=True)
            pe.wait_ge(mxt_go, 2)
            nc.tensor.matmul(ps[:, 7, 64:72], ones[0:8, :], diag[0:8, :], start=True, stop=True).then_inc(mxt_done, 1)
            slot(0, 3, first=True)
            for c in range(2, NCH):
                pe.wait_ge(s_xk[c], XK[c])
            with pe.Fori(1, NCH - 1) as c:
                for g in range(G):
                    slot(c, g)
            for g in range(G):
                slot(NCH - 1, g, last=True)
            pe.wait_ge(rb_ready, 2 * B)
            project(NCH - 1, 0, (0,))
            project(NCH - 1, 1, (0,), bank=6)
            project(NCH - 1, 0, (1, 2, 3))
            project(NCH - 1, 1, (1, 2, 3), bank=6)

            def largest(n):
                pe.wait_ge(gm_go, 2 * n + 1)
                nc.tensor.transpose(ps[0:1, 5, 0:P], mx[:, 8:9], ident[:]).then_inc(gm_done, 1)
                pe.wait_ge(gm_go, 2 * n + 2)
                nc.tensor.matmul(ps[:, 5, 0:1], ones[0:1, :], rowm[0:1, 0:1], start=True,
                                 stop=True).then_inc(gm_done, 1)

            def qconv(k, c, bank, done):
                for h in range(2):
                    pe.wait_ge(q_ready, 2 * (NCH * k + c) + h + 1)
                    for t in range(TAPS):
                        dy, dx = divmod(t, 3)
                        r0 = HALF_ROWS * h + dy
                        i = nc.tensor.matmul(ps[:, bank + h, :HALF], wqi[:, k, t, :],
                                             qi[:, c, r0:r0 + HALF_ROWS, dx:dx + W],
                                             start=(t == 0), stop=(t == TAPS - 1))
                    i.then_inc(done, 1)

            pe.wait_ge(wl_ready, 1)
            largest(0)
            for c in range(NCH):
                wait(pe, h1_ready, 2 * (c - 1))
                qconv(0, c, 2 * (c % 2), q1_done)
            largest(1)

            def lconv(layer, c):
                if c == 0:
                    pe.wait_ge(wst_ready, layer + 1)
                pe.wait_ge(s_dup[layer][c], 16)
                bank = 2 + 2 * layer
                if layer == 0:
                    wait(pe, yb_ready, DONE_BEFORE["c", c])
                else:
                    wait(pe, yb_ready, DONE_BEFORE["d", c])
                for h in range(2):
                    for t in range(TAPS):
                        dy, dx = divmod(t, 3)
                        r0 = HALF_ROWS * h + dy
                        for g in range(G):
                            i = nc.tensor.matmul(ps[C * g:C * g + C, bank + h, :HALF],
                                                 wst[:, layer, C * t:C * t + C],
                                                 kst[:, layer, c % 2, g, r0:r0 + HALF_ROWS, dx:dx + W],
                                                 start=(t == 0), stop=(t == TAPS - 1))
                i.then_inc(lconv_done[layer], 1)

            for kind, c in TAIL:
                if kind == "q":
                    wait(pe, t1_ready, c - 1)
                    qconv(1, c, QBANK[c % 2], q2_done)
                else:
                    lconv("cd".index(kind), c)

        @block.scalar
        def _(act):
            act.dma_start(w1r[:], w1).then_inc(s_w1, 16)
            act.dma_start(w2br[0:HB, :], w2b).then_inc(s_w2b, 16)
            act.dma_start(par[:], params).then_inc(s_par, 16)
            n = [0]

            def link(ins):
                n[0] += 1
                ins.then_inc(a_chain, 1)
                act.wait_ge(a_chain, n[0])

            act.wait_ge(pool_zeroed, 2)
            for k in range(3):
                dy = slice(3 * HID * k, 3 * HID * k + 3 * HID)
                act.wait_ge(s_w2a[k], 16)
                nc.scalar.activation(ajunk[:, dy], w2ar[:, dy], ACT.Abs,
                                     accum_out=cm[:, 0, 0:3, 1][:, k:k + 1]).then_inc(a_abs, 1)
            act.wait_ge(s_w2b, 16)
            link(nc.scalar.activation(wjunk[0:HB, :], w2br[0:HB, :], ACT.Abs,
                                      accum_out=col[0:HB, SB + 1:SB + 2]))
            act.wait_ge(a_abs, 3)
            nc.scalar.activation(cm[:, 1, 0:3, 1], cm[:, 0, 0:3, 1], ACT.Copy,
                                 accum_out=col[:, SUMS + 1:SUMS + 2]).then_inc(a_sum, 1)

            def relu_exp(j, n, b, bank=6):
                two, h = divmod(n, 2)
                done, ready, at = ((expa_done, ra_ready, BN1A), (expb_done, rb_ready, BN1B))[two]
                dst = raj[b][:, two, :]
                act.wait_ge(done, 2 * j + h + 1)
                if h == 0:
                    wait(act, (hp_done, hb_ready)[two], j - 1)
                nc.scalar.activation(dst[:, HALF * h:HALF * h + HALF], ps[:, bank, :HALF], ACT.Relu,
                                     bias=bn[:, BSH, at:at + 1], scale=bn[:, BSC, at:at + 1]).then_inc(ready, 1)

            def copy_m1(j):
                act.wait_ge(m_done, 4 * j + 1)
                wait(act, out_v, 3 * j - 2)
                nc.scalar.copy(c1a[:], ps[:, 1, :HALF]).then_inc(c1_ready, 1)

            def copy_y(j):
                act.wait_ge(convb_done, j + 1)
                wait(act, z_half, j)
                nc.scalar.mul(cy[0:HB, :], ps[HB:P, 4, :HALF], -1.0)
                nc.scalar.copy(cy[HB:P, :], ps[0:HB, 4, :HALF]).then_inc(cy_ready, 1)

            def hi(j, b):
                act.wait_ge(v_ready, j + 1)
                wait(act, convb_done, j - 1)
                nc.scalar.copy(vh[:, b, 0].rearrange("p k h w -> p (k h w)"),
                               va[:].rearrange("p k h w -> p (k h w)")).then_inc(vhi_ready, 1)

            def relu_a(j):
                act.wait_ge(out_v, 3 * j + 3)
                nc.scalar.activation(r2a[:], r2a[:], ACT.Relu, bias=bn[:, BSH, BN2A:BN2A + 1],
                                     scale=bn[:, BSC, BN2A:BN2A + 1]).then_inc(r2a_ready, 1)

            def relu_b(j):
                act.wait_ge(z_ready, j + 1)
                nc.scalar.activation(r2b[:], r2b[:], ACT.Relu, bias=bn[:, BSH, BN2B:BN2B + 1],
                                     scale=bn[:, BSC, BN2B:BN2B + 1]).then_inc(r2b_ready, 1)

            def add_shift(c):
                if isinstance(c, int) and c == 0:
                    act.wait_ge(bn_ready, 1)
                act.wait_ge(x_split, c + 1)
                nc.scalar.activation(xin[:, c, :], xin[:, c, :], ACT.Identity,
                                     bias=bn[:, BSH, BN3:BN3 + 1]).then_inc(xs_ready, 1)

            def slot(c, g, first=False, last=False):
                j = c * G + g
                begin = first and g == 0
                end = last and g == G - 1
                ahead = not last or g < G - 2
                if not begin:
                    copy_y(j - 1)
                if ahead:
                    relu_exp(j + 2, 0, g % 2)
                if not begin:
                    relu_b(j - 1)
                copy_m1(j)
                if ahead:
                    relu_exp(j + 2, 1, g % 2)
                if not end:
                    hi(j + 1, (g + 1) % 2)
                if begin:
                    act.wait_ge(thr_ready, 1)
                    nc.scalar.activation(ajunk, ajunk, ACT.Relu, bias=col[:, NDEL + 1:NDEL + 2],
                                         accum_out=col[:, PART1 + 1:PART1 + 2])
                    nc.scalar.activation(wjunk[0:HB, :], wjunk[0:HB, :], ACT.Relu, bias=col[0:HB, NDEL + 1:NDEL + 2],
                                         accum_out=col[0:HB, PART2 + 1:PART2 + 2]).then_inc(a_sum, 1)
                    act.wait_ge(a_sum, 2)
                    act.wait_ge(w2_ready, 3)
                    nc.scalar.activation(ajunk, w2at[:].rearrange("p t o -> p (t o)"), ACT.Square,
                                         accum_out=col[:, PART1 + 4:PART1 + 5]).then_inc(a_sum, 1)
                    nc.scalar.activation(wjunk[0:HB, :], w2bt[0:HB].rearrange("p t o -> p (t o)"), ACT.Square,
                                         accum_out=col[0:HB, PART2 + 4:PART2 + 5]).then_inc(a_sum, 1)
                if ahead:
                    relu_exp(j + 2, 2, g % 2)
                    relu_exp(j + 2, 3, g % 2)
                if begin:
                    act.wait_ge(bn_ready, 1)
                relu_a(j)
                if g == 1:
                    add_shift(c)

            act.wait_ge(bn1_ready, 1)
            for n in range(4):
                relu_exp(0, n, 0, bank=n)
            hi(0, 0)
            for n in range(4):
                relu_exp(1, n, 1)
            for g in range(G):
                slot(0, g, first=True)
            with act.Fori(1, NCH - 1) as c:
                for g in range(G):
                    slot(c, g)
            for g in range(G):
                slot(NCH - 1, g, last=True)
            copy_y(B - 1)
            relu_b(B - 1)

            ROWS = (slice(0, HALF_ROWS + 1), slice(HALF_ROWS + 1, H))

            def quant(c, k):
                for h, rows in enumerate(ROWS):
                    act.wait_ge(q_v, 2 * (NCH * k + c) + h + 1)
                    nc.scalar.activation(inner(qi[:, c])[:, rows], img(qf[:, c % 2, :])[:, rows], ACT.Copy,
                                         bias=-MAGIC).then_inc(q_ready, 1)

            def out1(c):
                for h in range(2):
                    act.wait_ge(q1_done, 2 * c + h + 1)
                    nc.scalar.activation(h1[:, c, HALF * h:HALF * h + HALF], ps[:, 2 * (c % 2) + h, :HALF], ACT.Relu,
                                         bias=bn[:, BSH, BNQ1:BNQ1 + 1],
                                         scale=col[:, SIG:SIG + 1]).then_inc(h1_ready, 1)

            act.wait_ge(pool_zeroed, 9)
            quant(0, 0)
            act.wait_ge(scale_ready, 1)
            for c in range(1, NCH):
                quant(c, 0)
                out1(c - 1)
            out1(NCH - 1)
            act.wait_ge(q1_done, 2 * NCH)
            for c in range(2):
                quant(c, 1)
            act.wait_ge(scale_ready, 2)
            for c in range(NCH):
                if c >= 2:
                    quant(c, 1)
                nc.scalar.activation(y0[:, c, :], y0[:, c, :], ACT.Identity, bias=col[:, SIG + 3:SIG + 4],
                                     scale=col[:, SIG + 2:SIG + 3]).then_inc(ys_ready, 1)

            def stack(layer, c):
                act.wait_ge(part_ready[layer], 2 * c + 2)
                wait(act, lconv_done[layer], c - 1)
                for i, (g, k) in enumerate(A_SHARE):
                    ins = nc.scalar.copy(kst[C * k:C * k + C, layer, c % 2, g],
                                         part[C * g:C * g + C, layer, c % 2, k])
                ins.then_inc(stack_a[layer], 1)

            def relu_l(layer, c):
                act.wait_ge(lconv_done[layer], c + 1)
                k = BNC + layer
                n = LTAIL.index(("cd"[layer], c))
                if n >= 2:
                    k2, c2 = LTAIL[n - 2]
                    act.wait_ge(*((part_ready[1], 2 * c2 + 2) if k2 == "c" else (o_ready, c2 + 1)))
                b = 2 + 2 * layer
                nc.scalar.activation(img(yb[:, n % 2, :], 2), ps[:, b:b + 2, :HALF], ACT.Relu,
                                     bias=bn[:, BSH, k:k + 1],
                                     scale=col[:, SIG + 4 + layer:SIG + 5 + layer]).then_inc(yb_ready, 1)

            for kind, c in TAIL:
                if kind == "q":
                    stack(0, c)
                else:
                    relu_l("cd".index(kind), c)
                    if kind == "c":
                        stack(1, c)

        @block.vector
        def _(dve):
            n = [0]

            def link(ins):
                n[0] += 1
                ins.then_inc(v_chain, 1)
                dve.wait_ge(v_chain, n[0])

            def c1(k, p=P, w=1):
                return col[0:p, k:k + w]

            ts, tt, stt = nc.vector.tensor_scalar, nc.vector.tensor_tensor, nc.vector.scalar_tensor_tensor

            def ternary(raw, out_, neg, k, p, cols):
                link(ts(neg, raw, c1(NDEL + k, p), None, ALU.is_lt))
                return stt(out_, raw, c1(DEL + k, p), neg, ALU.is_gt, ALU.subtract)

            def threshold(k, n, count, at=0):
                link(ts(c1(DEL + k), ps[:, TOTAL_BANK[n], 8 * n + at:8 * n + at + 1], 1.0 / count, 0.7, ALU.mult, ALU.mult))
                link(ts(c1(NDEL + k), c1(DEL + k), -1.0, None, ALU.mult))

            def alphas(k, w, at, at2):
                link(ts(c1(TMP, w=w), ps[:, TOTAL_BANK[2], at2:at2 + w], 1.0, None, ALU.max))
                link(nc.vector.reciprocal(c1(TMP, w=w), c1(TMP, w=w)))
                link(tt(c1(AL + k, w=w), c1(TMP, w=w), ps[:, TOTAL_BANK[2], at:at + w], ALU.mult))

            dve.wait_ge(pool_zeroed, 2)
            dve.wait_ge(s_w1, 16)
            nc.vector.tensor_reduce(c1(SUMS, C), w1r[:], AX.X, ALU.add, apply_absolute_value=True).then_inc(sums_ready, 1)

            dve.wait_ge(s_x[0], 16)
            xb = [xpart[:, 0, k, :] for k in range(3)]
            link(nc.vector.tensor_copy(xb[0], xin[:, 0, :]))
            link(tt(xrest[:, 0, :], xin[:, 0, :], xb[0], ALU.subtract))
            link(nc.vector.tensor_copy(xb[1], xrest[:, 0, :]))
            link(tt(xrest[:, 1, :], xrest[:, 0, :], xb[1], ALU.subtract))
            nc.vector.tensor_copy(xb[2], xrest[:, 1, :]).then_inc(x_split, 1)
            dve.wait_ge(x_split, 1)
            for k in range(3):
                i = nc.vector.tensor_copy(xk[C * k:C * k + C, 0, :], xpart[0:C, 0, k, :])
            i.then_inc(x0_ready, 1)

            dve.wait_ge(sums_done, 1)
            threshold(0, 1, N1)
            link(ternary(w1r[:], w1t[0:C, 0:HID], wneg[0:C, 0:HID], 0, C, HID))
            link(nc.vector.tensor_copy(w1t[0:C, HID:HID + HB], w1t[0:C, P:HID]))
            for k in (1, 2):
                i = nc.vector.tensor_copy(w1t[C * k:C * k + C, :], w1t[0:C, :])
            i.then_inc(w1_ready, 1)
            stt(r2a[0:C, 0:HID], w1r[:], 1.0, w1t[0:C, 0:HID], ALU.mult, ALU.mult, accum_out=c1(PART1, C))
            stt(r2a[0:C, HID:2 * HID], w1t[0:C, 0:HID], 1.0, w1t[0:C, 0:HID], ALU.mult, ALU.mult,
                accum_out=c1(PART1 + 3, C)).then_inc(sums_ready, 1)
            dve.wait_ge(s_w3, 48)
            nc.vector.tensor_reduce(c1(SUMS + 2), w3r[:, 0, :], AX.X, ALU.add, apply_absolute_value=True)
            nc.vector.tensor_reduce(c1(SB + 2, HB), w3r[0:HB, 1, :], AX.X, ALU.add,
                                    apply_absolute_value=True).then_inc(w3s_ready, 1)
            dve.wait_ge(sums_done, 2)
            alphas(0, 1, 16, 17)
            dve.wait_ge(inv_ready, 1)
            ts(bn[:, BSC, BN1A:BN2A], bn[:, BSC, BN1A:BN2A], c1(AL), S0, ALU.mult, ALU.mult).then_inc(bn1_ready, 1)

            flat = "p t o -> p (t o)"
            DY = 3 * HID

            def w2_rows():
                dve.wait_ge(sums_done, 3)
                link(ts(c1(DEL + 1), ps[:, TOTAL_BANK[3], 24:25], 1.0 / N2, 0.7, ALU.mult, ALU.mult))
                ts(c1(NDEL + 1), c1(DEL + 1), -1.0, None, ALU.mult).then_inc(thr_ready, 1)
                dve.wait_ge(thr_ready, 1)
                link(ts(wneg, w2ar, c1(NDEL + 1), None, ALU.is_lt))
                for k in (0, 2, 1):
                    dy = slice(DY * k, DY * k + DY)
                    i = stt(w2at[:].rearrange(flat)[:, dy], w2ar[:, dy], c1(DEL + 1), wneg[:, dy],
                            ALU.is_gt, ALU.subtract)
                    if k == 2:
                        i.then_inc(w2_ready, 1)
                    if k == 1:
                        link(i)

            def w2_transforms():
                t = w2at[:].rearrange(flat)
                u = wu[:].rearrange("p k d o -> p k (d o)")
                g = [t[:, DY * k:DY * k + DY] for k in range(3)]
                link(tt(wneg[:, 0:DY], g[0], g[2], ALU.add))
                tt(u[:, 0], wneg[:, 0:DY], g[1], ALU.add)
                link(tt(u[:, 1], wneg[:, 0:DY], g[1], ALU.subtract))
                link(ts(wu[:].rearrange("p k d o -> p (k d o)"), wu[:].rearrange("p k d o -> p (k d o)"), 0.5, None, ALU.mult))
                ts(wun[:], wu[:, 1, :, P:HID], -1.0, None, ALU.mult).then_inc(w2_ready, 1)

            def w2_rest():
                t = w2bt[:].rearrange(flat)
                dve.wait_ge(w2_ready, 2)
                link(ternary(w2br[0:HB, :], t[0:HB], wneg[0:HB, :], 1, HB, None))
                nc.vector.tensor_copy(t[HB:P], t[0:HB]).then_inc(w2_ready, 1)

            def clamp(j, b):
                dve.wait_ge(ra_ready, 2 * j + 2)
                if isinstance(j, int) and j == 0:
                    dve.wait_ge(pool_zeroed, 4)
                ts(inner(hp), img(raj[b][:, 0, :]), CAP, None, ALU.min).then_inc(hp_done, 1)
                dve.wait_ge(hp_done, j + 1)

            def transforms(j):
                wait(dve, vhi_ready, j)
                d = [hp[:, k:k + 2 * TR - 1:2, :] for k in range(4)]
                for k, (x0, x1, op) in enumerate(((0, 2, ALU.subtract), (1, 2, ALU.add), (2, 1, ALU.subtract),
                                                  (3, 1, ALU.subtract))):
                    i = tt(va[:, k], d[x0], d[x1], op)
                i.then_inc(v_ready, 1)

            def lo(j, b):
                dve.wait_ge(vhi_ready, j + 1)
                v = "p k h w -> p (k h w)"
                tt(vh[:, b, 1].rearrange(v), va[:].rearrange(v), vh[:, b, 0].rearrange(v),
                   ALU.subtract).then_inc(va_ready, 1)

            def halves_b(j, b):
                dve.wait_ge(rb_ready, 2 * j + 2)
                wait(dve, convb_done, j - 1)
                if isinstance(j, int) and j == 0:
                    dve.wait_ge(pool_zeroed, 6)
                ts(inner(hb[:, b]), img(raj[b][:, 1, :]), CAP, None, ALU.min).then_inc(hbhi_done, 1)
                dve.wait_ge(hbhi_done, j + 1)
                up = slice(HB, P)
                low = hb[up, b, 1:1 + H, 1:1 + W]
                stt(low, img(raj[b][:, 1, :])[up], CAP, low, ALU.min,
                    ALU.subtract).then_inc(hb_ready, 1)

            def out_12(j):
                dve.wait_ge(c1_ready, j + 1)
                dve.wait_ge(m_done, 4 * j + 2)
                tt(ds[:, 0, :], c1a[:], ps[:, 2, :HALF], ALU.add)
                tt(ds[:, 1, :], c1a[:], ps[:, 2, :HALF], ALU.subtract).then_inc(out_v, 1)

            def out_row(j, odd):
                dve.wait_ge(m_done, 4 * j + 3 + odd)
                dve.wait_ge(out_v, 3 * j + 1)
                tt(by_rows(r2a[:], odd), img(ds[:, odd, :], TR),
                   img(ps[:, 3 * odd, :HALF], TR), ALU.add).then_inc(out_v, 1)

            def out_b(j):
                dve.wait_ge(cy_ready, j + 1)
                tt(r2b[:], cy[:], ps[:, 4, :HALF], ALU.add).then_inc(z_half, 1)
                dve.wait_ge(z_half, j + 1)
                tt(r2b[:], r2b[:], ps[:, 5, :HALF], ALU.add).then_inc(z_ready, 1)

            def halves2_a(j, g):
                dve.wait_ge(r2a_ready, j + 1)
                ts(h2a[:, g, 0, :], r2a[:], CAP, None, ALU.min).then_inc(h2hi_done, 1)
                dve.wait_ge(h2hi_done, 2 * j + 1)
                stt(h2a[:, g, 1, :], r2a[:], CAP, h2a[:, g, 0, :], ALU.min, ALU.subtract).then_inc(h2a_ready, 1)

            def halves2_b(j, g):
                dve.wait_ge(r2b_ready, j + 1)
                ts(h2b[:, g, 0, :], r2b[:], CAP, None, ALU.min).then_inc(h2hi_done, 1)
                dve.wait_ge(h2hi_done, 2 * j + 2)
                stt(h2b[:, g, 1, :], r2b[:], CAP, h2b[:, g, 0, :], ALU.min, ALU.subtract).then_inc(h2_ready, 1)

            def residual(c, h, bank=7):
                dve.wait_ge(proj_done, 2 * c + h + 1)
                dve.wait_ge(xs_ready, c + 1)
                rows = by_rows(y0[:, c, :], h)
                stt(rows, img(ps[:, bank, :HALF], TR), bn[:, BSC, BN3:BN3 + 1], by_rows(xin[:, c, :], h),
                    ALU.mult, ALU.add).then_inc(y0_ready, 1)
                dve.wait_ge(y0_ready, 2 * c + h + 1)
                nc.vector.tensor_reduce(cm[:, 0, c, h:h + 1], rows, AX.XY, ALU.max).then_inc(cmax_done, 1)

            def slot(c, g, first=False, last=False):
                j = c * G + g
                begin = first and g == 0
                end = last and g == G - 1
                if not end:
                    clamp(j + 1, (g + 1) % 2)
                    transforms(j + 1)
                if not begin:
                    out_b(j - 1)
                    if g == 1:
                        wait(dve, proj_done, 2 * c)
                    halves2_a(j - 1, (g - 1) % G)
                    out_12(j)
                    halves2_b(j - 1, (g - 1) % G)
                else:
                    out_12(j)
                    w3_rest()
                if not end:
                    lo(j + 1, (g + 1) % 2)
                out_row(j, 0)
                if g == 0 and not first:
                    residual(c - 1, 0)
                if not end:
                    halves_b(j + 1, (g + 1) % 2)
                out_row(j, 1)
                if g == 0 and not first:
                    residual(c - 1, 1)

            def w3_rest():
                threshold(2, 3, N3, 1)
                ternary(w3r[:].rearrange("p k o -> p (k o)"), w3t[:].rearrange("p k o -> p (k o)"),
                        wneg[:, 0:2 * C], 2, P, None).then_inc(w3_ready, 1)
                dve.wait_ge(w3_ready, 1)
                junk = r2b[:]
                stt(junk[:, 0:C], w3r[:, 0, :], 1.0, w3t[:, 0, :], ALU.mult, ALU.mult, accum_out=c1(PART1 + 2))
                stt(junk[:, C:2 * C], w3t[:, 0, :], 1.0, w3t[:, 0, :], ALU.mult, ALU.mult, accum_out=c1(PART1 + 5))
                stt(junk[0:HB, 2 * C:3 * C], w3r[0:HB, 1, :], 1.0, w3t[0:HB, 1, :], ALU.mult, ALU.mult,
                    accum_out=c1(PART2 + 2, HB))
                stt(junk[0:HB, 3 * C:4 * C], w3t[0:HB, 1, :], 1.0, w3t[0:HB, 1, :], ALU.mult, ALU.mult,
                    accum_out=c1(PART2 + 5, HB)).then_inc(sums_ready, 1)
                dve.wait_ge(sums_done, 4)
                link(tt(c1(TMP), ps[:, 7, 36:37], c1(DEL + 1), ALU.mult))
                link(tt(c1(TMP + 2), c1(TMP), ps[:, 7, 33:34], ALU.add))
                link(nc.vector.tensor_copy(c1(TMP + 3), ps[:, 7, 34:35]))
                link(ts(c1(TMP, w=2), ps[:, 7, 36:38], 1.0, None, ALU.max))
                link(nc.vector.reciprocal(c1(TMP, w=2), c1(TMP, w=2)))
                link(tt(c1(AL + 1, w=2), c1(TMP, w=2), c1(TMP + 2, w=2), ALU.mult))
                link(ts(bn[:, BSC, BN2A:BN3], bn[:, BSC, BN2A:BN3], c1(AL + 1), None, ALU.mult))
                ts(bn[:, BSC, BN3:BN3 + 1], bn[:, BSC, BN3:BN3 + 1], c1(AL + 2), 1.0 / S0, ALU.mult,
                   ALU.mult).then_inc(bn_ready, 1)

            w2_rows()
            clamp(0, 0)
            transforms(0)
            lo(0, 0)
            w2_transforms()
            w2_rest()
            halves_b(0, 0)
            slot(0, 0, first=True)

            dve.wait_ge(s_wq, 16 * 2 * G)
            dve.wait_ge(s_wc, 16 * 2 * G)
            red = nc.vector.tensor_reduce
            for k in range(2):
                red(mx[:, MW1 + k:MW1 + k + 1], wqr[:, k, :], AX.X, ALU.max, apply_absolute_value=True)
                red(mx[:, MC + k:MC + k + 1], wcr[:, k, :], AX.X, ALU.max, apply_absolute_value=True)
            for m, kk, col_ in ((MI2, BSC, BNQ2), (MH2, BSH, BNQ2), (MIC, BSC, BNC), (MHC, BSH, BNC)):
                i = red(mx[:, m:m + 1], bn[:, kk, col_:col_ + 1], AX.X, ALU.max, apply_absolute_value=True)
            i.then_inc(mxt_go, 1)
            slot(0, 1, first=True)
            dve.wait_ge(mxt_done, 1)
            link(red(rowm[0:8, 1:2], ps[0:8, 7, P:2 * P], AX.X, ALU.max))
            dve.wait_ge(pool_ident, 1)
            ts(diag[0:8, :], ident[0:8, 0:8], rowm[0:8, 1:2], None, ALU.mult).then_inc(mxt_go, 1)
            slot(0, 2, first=True)
            dve.wait_ge(mxt_done, 2)
            link(nc.vector.tensor_copy(mxa[:], ps[:, 7, 64:72]))
            SW, RSW = 50, 52
            link(ts(c1(SW, w=2), mxa[:, MW1:MW1 + 2], 1e-8, 1.0 / WQ, ALU.max, ALU.mult))
            link(nc.vector.reciprocal(c1(RSW, w=2), c1(SW, w=2)))
            dve.wait_ge(pool_zeroed, 9)
            def integers(k):
                link(ts(wqq[:, k, :], wqr[:, k, :], c1(RSW + k), MAGIC, ALU.mult, ALU.add))
                link(ts(wqq[:, k, :], wqq[:, k, :], MAGIC - WQ, MAGIC + WQ, ALU.max, ALU.min))
                for g in range(G):
                    q = slice(C * g, C * g + C)
                    ts(wqi[q, k, :, C * g:C * g + C], wqq[q, k, :].rearrange("p (t o) -> p t o", t=TAPS),
                       -MAGIC, None, ALU.add)

            integers(0)
            slot(0, 3, first=True)
            integers(1)
            PWR, IPW = 54, 56
            link(ts(c1(PWR, w=2), mxa[:, MC:MC + 2], 1e-30, None, ALU.max))
            link(ts(c1(PWR, w=2).bitcast(I32), c1(PWR, w=2).bitcast(I32), 0x7F800000, None, ALU.bitwise_and))
            link(nc.vector.reciprocal(c1(IPW, w=2), c1(PWR, w=2)))
            KK = 58
            link(tt(c1(KK), mxa[:, MW2:MW2 + 1], mxa[:, MI2:MI2 + 1], ALU.mult))
            link(ts(c1(KK), c1(KK), float(TAPS * C), None, ALU.mult))
            link(tt(c1(KK + 1), mxa[:, MC:MC + 1], mxa[:, MIC:MIC + 1], ALU.mult))
            ts(c1(KK + 1), c1(KK + 1), float(TAPS * C), None, ALU.mult).then_inc(wl_ready, 1)


            def halves_w(k):
                link(ts(wcr[:, k, :], wcr[:, k, :], c1(IPW + k), F16_TOP, ALU.mult, ALU.mult))
                link(nc.vector.tensor_copy(wst[:, k, :], wcr[:, k, :]))
                up = slice(2 * C, P)
                tt(wst[up, k, :], wcr[up, k, :], wst[up, k, :], ALU.subtract).then_inc(wst_ready, 1)

            with dve.Fori(1, NCH - 1) as c:
                for g in range(G):
                    slot(c, g)
            for g in range(G):
                slot(NCH - 1, g, last=True)
            halves2_a(B - 1, G - 1)
            out_b(B - 1)
            halves2_b(B - 1, G - 1)
            residual(NCH - 1, 0)
            residual(NCH - 1, 1, bank=6)

            GM, RS, SA, BD = 36, 38, 42, 60

            def step(k):
                dve.wait_ge(cmax_done, 2 * NCH * (k + 1))
                red(mx[:, 8:9], cm[:, k].rearrange("p c h -> p (c h)"), AX.X, ALU.max).then_inc(gm_go, 1)
                dve.wait_ge(gm_done, 2 * k + 1)
                red(rowm[0:1, 0:1], ps[0:1, 5, 0:P], AX.X, ALU.max).then_inc(gm_go, 1)
                dve.wait_ge(gm_done, 2 * k + 2)
                link(ts(c1(GM + k), ps[:, 5, 0:1], 1e-8, None, ALU.max))
                link(ts(c1(SA + k), c1(GM + k), 1.0 / XQ, None, ALU.mult))
                link(nc.vector.reciprocal(c1(RS + k), c1(SA + k)))

            def quant(c, k, src):
                wait(dve, q_ready, 2 * (NCH * k + c - 1))
                for px in (slice(0, HALF + W), slice(HALF + W, HW)):
                    link(ts(qf[:, c % 2, px], src[:, c, px], c1(RS + k), MAGIC, ALU.mult, ALU.add))
                    ts(qf[:, c % 2, px], qf[:, c % 2, px], MAGIC, MAGIC + XQ, ALU.max, ALU.min).then_inc(q_v, 1)

            step(0)
            quant(0, 0, y0)
            quant(1, 0, y0)
            link(tt(c1(TMP), c1(SA), c1(SW), ALU.mult))
            tt(c1(SIG), c1(TMP), bn[:, BSC, BNQ1:BNQ1 + 1], ALU.mult).then_inc(scale_ready, 1)
            for c in range(2, NCH):
                quant(c, 0, y0)
            halves_w(0)
            halves_w(1)
            for c in range(NCH):
                for h in range(2):
                    dve.wait_ge(h1_ready, 2 * c + h + 1)
                    red(cm[:, 1, c, h:h + 1], h1[:, c, HALF * h:HALF * h + HALF], AX.X,
                        ALU.max).then_inc(cmax_done, 1)
            step(1)
            quant(0, 1, h1)
            quant(1, 1, h1)
            link(tt(c1(TMP), c1(SA + 1), c1(SW + 1), ALU.mult))
            link(tt(c1(SIG + 1), c1(TMP), bn[:, BSC, BNQ2:BNQ2 + 1], ALU.mult))
            link(stt(c1(BD), c1(GM + 1), c1(KK), mxa[:, MH2:MH2 + 1], ALU.mult, ALU.add))
            link(tt(c1(BD), c1(BD), c1(GM), ALU.add))
            link(stt(c1(BD + 1), c1(BD), c1(KK + 1), mxa[:, MHC:MHC + 1], ALU.mult, ALU.add))
            link(ts(c1(BD, w=2), c1(BD, w=2), 1e-30, None, ALU.max))
            link(ts(c1(BD, w=2).bitcast(I32), c1(BD, w=2).bitcast(I32), 0x7F800000, None, ALU.bitwise_and))
            link(nc.vector.reciprocal(c1(BD + 2, w=2), c1(BD, w=2)))
            link(ts(c1(BD + 2, w=2), c1(BD + 2, w=2), F16_TOP, None, ALU.mult))
            link(tt(c1(SIG + 1), c1(SIG + 1), c1(BD + 2), ALU.mult))
            link(ts(c1(SIG + 2), c1(BD + 2), 1.0, None, ALU.mult))
            link(tt(c1(SIG + 3), c1(BD + 2), bn[:, BSH, BNQ2:BNQ2 + 1], ALU.mult))
            for k in range(2):
                link(tt(c1(TMP + k), c1(BD + k), c1(PWR + k), ALU.mult))
                link(ts(c1(TMP + k), c1(TMP + k), F16_TOP ** -2, None, ALU.mult))
                i = tt(c1(SIG + 4 + k), c1(TMP + k), bn[:, BSC, BNC + k:BNC + k + 1], ALU.mult)
            i.then_inc(scale_ready, 1)
            for c in range(2, NCH):
                quant(c, 1, h1)

            def stack(layer, c):
                dve.wait_ge(part_ready[layer], 2 * c + 2)
                wait(dve, lconv_done[layer], c - 1)
                for g, k in V_SHARE:
                    i = nc.vector.tensor_copy(kst[C * k:C * k + C, layer, c % 2, g].rearrange("p h w -> p (h w)"),
                                              part[C * g:C * g + C, layer, c % 2, k].rearrange("p h w -> p (h w)"))
                i.then_inc(stack_v[layer], 1)

            def split(layer, c, src, scale, op):
                if layer == 1 and c == 0:
                    dve.wait_ge(pool_zeroed, 10)
                if c >= 2:
                    dve.wait_ge(stack_a[layer], c - 1)
                hi, lo = (inner(part[:, layer, c % 2, k]) for k in range(2))
                ts(hi, src, scale, None, op).then_inc(part_ready[layer], 1)
                dve.wait_ge(part_ready[layer], 2 * c + 1)
                stt(lo, src, scale, hi, op, ALU.subtract).then_inc(part_ready[layer], 1)
                stack(layer, c)

            def cut(layer, c):
                n = LTAIL.index(("cd"[layer], c))
                dve.wait_ge(yb_ready, n + 1)
                m = cm[:, layer, c, 1:2]
                link(red(m, yb[:, n % 2, :], AX.X, ALU.max))
                if layer == 0:
                    link(ts(m, m, CUT, c1(BD + 3), ALU.is_ge, ALU.mult))
                    split(1, c, img(yb[:, n % 2, :]), m, ALU.mult)
                else:
                    link(ts(m, m, CUT, None, ALU.is_ge))
                    ts(om[:, c, :], yb[:, n % 2, :], m, None, ALU.mult).then_inc(o_ready, 1)

            steps = list(TAIL)
            for i, (kind, c) in enumerate(steps):
                if kind == "q":
                    dve.wait_ge(q2_done, 2 * (c + 1))
                    dve.wait_ge(ys_ready, c + 1)
                    qb = QBANK[c % 2]
                    stt(img(t1[:, c % 2, :], 2), ps[:, qb:qb + 2, :HALF], c1(SIG + 1), img(y0[:, c, :], 2),
                        ALU.mult, ALU.add).then_inc(t1_ready, 1)
                    dve.wait_ge(t1_ready, c + 1)
                    split(0, c, img(t1[:, c % 2, :]), 0.0, ALU.max)
                else:
                    cut("cd".index(kind), c)


def kernel(**inputs):
    import numpy as np
    import concourse.bacc as bacc
    from concourse.bass_utils import run_bass_kernel_spmd

    a = {k: np.asarray(v) for k, v in inputs.items()}

    def blocks(v):
        return np.ascontiguousarray(v.reshape(NCH, G, C, HW).transpose(1, 2, 0, 3).reshape(P, NCH, HW))

    def taps_first(w):
        return np.ascontiguousarray(w.transpose(1, 2, 3, 0).reshape(w.shape[1], -1))

    def column(kind):
        names = {"g": ("L1_conv_bn%d_gamma", "gamma"), "b": ("L1_conv_bn%d_beta", "beta"),
                 "m": ("L1_conv_bn%d_mean", "run_mean"), "v": ("L1_conv_bn%d_var", "run_var")}[kind]
        cols = []
        for k in (1, 2):
            v = a[f"L0_conv_{kind}{k}"]
            cols += [v[:P], np.tile(v[P:], 2)]
        cols.append(np.tile(a[f"L0_conv_{kind}3"], G))
        cols += [np.tile(a[names[0] % k], G) for k in (1, 2)]
        cols += [np.tile(a[f"L{k}_conv_{names[1]}"], G) for k in (2, 3)]
        return cols

    params = np.stack([c for kind in "gbmv" for c in column(kind)]
                      + [np.tile(a[f"L{k}_conv_conv_b"], G) for k in (2, 3)], axis=1)
    w2 = taps_first(a["L0_conv_w2"])
    arrays = {
        "x_in": blocks(a["x"]), "params_in": np.ascontiguousarray(params),
        "w1_in": taps_first(a["L0_conv_w1"]), "w2a_in": w2[:P], "w2b_in": np.ascontiguousarray(w2[P:]),
        "w3_in": taps_first(a["L0_conv_w3"]), "wq1_in": taps_first(a["L1_conv_w1"]),
        "wq2_in": taps_first(a["L1_conv_w2"]), "wc_in": taps_first(a["L2_conv_conv_w"]),
        "wd_in": taps_first(a["L3_conv_conv_w"]),
    }
    nc = bacc.Bacc("TRN2", target_bir_lowering=False, num_devices=1)
    args = [nc.dram_tensor(n, v.shape, F32, kind="ExternalInput").ap() for n, v in arrays.items()]
    out = nc.dram_tensor("y_out", (P, NCH, HW), F32, kind="ExternalOutput").ap()
    conv_seq(nc, *args, out)
    r = run_bass_kernel_spmd(nc, [arrays], core_ids=[0])
    y = np.asarray(r.results[0]["y_out"])
    return np.ascontiguousarray(y.reshape(G, C, NCH, H, W).transpose(2, 0, 1, 3, 4).reshape(B, C, H, W))
```

```python
from contextlib import ExitStack

import concourse.bass as bass
from concourse import mybir

P = 128
B, C, H, W = 16, 32, 28, 28
HID = 192
G = P // C
NCH = B // G
HW = H * W
HALF_ROWS = H // 2
HALF = HALF_ROWS * W
PW = W + 2
PAD = (H + 2) * PW
TAPS = 9
TR = H // 2
HB = HID - P
EPS = 1e-5
CUT = 1e-3
S0 = 4096.0
CAP = 6.0 * S0
MAGIC = 1.5 * 2.0 ** 23
XQ = 255.0
WQ = 127.0
F16_TOP = 2.0 ** 14

F32 = mybir.dt.float32
F16 = mybir.dt.float16
BF16 = mybir.dt.bfloat16
I32 = mybir.dt.int32
ALU = mybir.AluOpType
ACT = mybir.ActivationFunctionType
AX = mybir.AxisListType

BN1A, BN1B, BN2A, BN2B, BN3, BNQ1, BNQ2, BNC, BND = range(9)
NBN = 9
KG, KB, KM, KV = range(4)
NPAR = 4 * NBN + 2

TAIL = [("q", 0), ("q", 1), ("q", 2), ("c", 0), ("q", 3), ("c", 1), ("d", 0), ("c", 2), ("d", 1),
        ("c", 3), ("d", 2), ("d", 3)]
A_SHARE = [(0, 0), (1, 0)]
V_SHARE = [(g, k) for k in range(2) for g in range(G) if (g, k) not in A_SHARE]
V_DUP = [(0, 0), (1, 0), (1, 1), (1, NCH - 1)]
XK = [16 * 3 * (G - 2)] + [16 * 3 * G] * (NCH - 1)
TOTAL_BANK = {1: 4, 2: 5, 3: 7, 4: 7, 5: 7}
QBANK = (0, 6)
LTAIL = [s for s in TAIL if s[0] != "q"]
DONE_BEFORE = {(k, c): (LTAIL.index((k, c - 1)) + 1 if c else 0) for k, c in LTAIL}

N1, N2, N3 = C * HID, HID * HID * TAPS, HID * C


def conv_seq(nc, x, params, w1, w2a, w2b, w3, wq1, wq2, wc, wd, out):
    with ExitStack() as ctx:
        def sb(name, shape, dt):
            return ctx.enter_context(nc.sbuf_tensor(name, shape, dt))

        def sem(name):
            return ctx.enter_context(nc.semaphore(name))

        par = sb("par", [P, NPAR], F32)
        xin = sb("xin", [P, NCH, HW], F32)
        w1r = sb("w1r", [C, HID], F32)
        big = sb("big", [P, 5, TAPS * HID], F32)
        w2ar, w2br, wjunk, ajunk = (big[:, k, :] for k in range(4))
        wneg = big[:, 4, :].bitcast(F16)[:, 0:TAPS * HID]
        kst = big[:].rearrange("p k f -> p (k f)").bitcast(F16)[:, 0:4 * G * PAD].rearrange(
            "p (l b g h w) -> p l b g h w", l=2, b=2, g=G, h=H + 2)
        w3r = sb("w3r", [P, 2, C], F32)
        wqr = sb("wqr", [P, 2, TAPS * C], F32)
        wcr = sb("wcr", [P, 2, TAPS * C], F32)
        w1t = sb("w1t", [96, HID + HB], BF16)
        w2at = sb("w2at", [P, TAPS, HID], F16)
        w2bt = sb("w2bt", [P, TAPS, HID], F16)
        w3t = sb("w3t", [P, 2, C], F16)
        xpart = sb("xpart", [P, 2, 3, HW], BF16)
        xrest = sb("xrest", [P, 2, HW], F32)
        xk = sb("xk", [96, B, HW], BF16)
        ra = sb("ra", [P, 2, HW], F32)
        hp = sb("hp", [P, H + 2, PW], F32)
        va = sb("va", [P, 4, TR, PW], F32)
        vh = sb("vh", [P, 2, 2, 4, TR, PW], F16)
        hb = sb("hb", [P, 2, H + 2, PW], F16)
        wu = sb("wu", [P, 2, 3, HID], F16)
        wun = sb("wun", [P, 3, HB], F16)
        c1a = sb("c1a", [P, HALF], F32)
        ds = sb("ds", [P, 2, HALF], F32)
        cy = sb("cy", [P, HALF], F32)
        r2a = sb("r2a", [P, HW], F32)
        r2b = sb("r2b", [P, HALF], F32)
        h2a = sb("h2a", [P, G, 2, HW], F16)
        h2b = sb("h2b", [P, G, 2, HALF], F16)
        y0 = sb("y0", [P, NCH, HW], F32)
        col = sb("col", [P, 74], F32)
        magic = sb("magic", [P, 2], F32)
        keep = sb("keep", [P, 2 * NCH], F32)
        bn = sb("bn", [P, 8, NBN], F32)
        mx = sb("mx", [P, 16], F32)
        expo = sb("expo", [P, NBN], F32)
        ident = sb("ident", [P, P], F32)
        ones = sb("ones", [P, P], F32)
        rowm = sb("rowm", [P, 4], F32)
        diag = sb("diag", [P, 8], F32)
        mxa = sb("mxa", [P, 8], F32)
        wqq = sb("wqq", [P, 2, TAPS * C], F32)
        wqi = sb("wqi", [P, 2, TAPS, P], BF16)
        wst = sb("wst", [P, 2, TAPS * C], F16)
        qf = ra
        qi = sb("qi", [P, NCH, H + 2, PW], BF16)
        h1 = h2a[:].rearrange("p g k f -> p g (k f)").bitcast(F32)
        t1 = va[:].rearrange("p k h w -> p (k h w)")[:, 0:2 * HW].rearrange("p (b f) -> p b f", b=2)
        yb = vh[:].rearrange("p b s k h w -> p (b s k h w)").bitcast(F32)[:, 0:2 * HW].rearrange(
            "p (b f) -> p b f", b=2)
        part = sb("part", [P, 2, 2, 2, H + 2, PW], F16)
        raj = [ra[:], part[:, 1].rearrange("p b k h w -> p (b k h w)").bitcast(F32)[:, 0:2 * HW].rearrange(
            "p (b f) -> p b f", b=2)]
        om = xin
        cm = sb("cm", [P, 2, NCH, 2], F32)

        ps = ctx.enter_context(nc.psum_tensor("ps", [P, 8, 512], F32))

        s_par, s_w1, s_w2b, s_w3, s_wq, s_wc = map(sem, ("s_par", "s_w1", "s_w2b", "s_w3", "s_wq", "s_wc"))
        s_w2a = [sem(f"s_w2a{k}") for k in range(3)]
        s_x = [sem(f"s_x{c}") for c in range(NCH)]
        s_ximg1 = sem("s_ximg1")
        s_xk = [sem(f"s_xk{c}") for c in range(NCH)]
        s_dup = [[sem(f"s_dup{l}_{k}") for k in range(NCH)] for l in range(2)]
        s_out = sem("s_out")

        v_chain, a_chain, pool_chain = map(sem, ("v_chain", "a_chain", "pool_chain"))

        pool_zeroed, pool_ident, x_split = map(sem, ("pool_zeroed", "pool_ident", "x_split"))
        sums_ready, w3s_ready, a_abs, a_sum, sums_done = map(
            sem, ("sums_ready", "w3s_ready", "a_abs", "a_sum", "sums_done"))
        thr_ready, w1_ready, w2_ready, w3_ready = map(sem, ("thr_ready", "w1_ready", "w2_ready", "w3_ready"))
        inv_ready, bn1_ready, bn_ready = map(sem, ("inv_ready", "bn1_ready", "bn_ready"))
        mxt_go, mxt_done, ws_ready, wl_ready, wst_ready = map(
            sem, ("mxt_go", "mxt_done", "ws_ready", "wl_ready", "wst_ready"))

        expa_done, expb_done, m_done, convb_done, proj_done = map(
            sem, ("expa_done", "expb_done", "m_done", "convb_done", "proj_done"))
        ra_ready, rb_ready, vhi_ready, c1_ready, cy_ready, r2a_ready, r2b_ready, xs_ready = map(
            sem, ("ra_ready", "rb_ready", "vhi_ready", "c1_ready", "cy_ready", "r2a_ready", "r2b_ready",
                  "xs_ready"))
        x0_ready, hp_done, v_ready, va_ready, hbhi_done, hb_ready = map(
            sem, ("x0_ready", "hp_done", "v_ready", "va_ready", "hbhi_done", "hb_ready"))
        out_v, z_half, z_ready, h2hi_done, h2a_ready, h2_ready, y0_ready = map(
            sem, ("out_v", "z_half", "z_ready", "h2hi_done", "h2a_ready", "h2_ready", "y0_ready"))

        cmax_done, gm_go, gm_done, scale_ready = map(sem, ("cmax_done", "gm_go", "gm_done", "scale_ready"))
        q_v, q_ready, q1_done, h1_ready, q2_done, ys_ready, t1_ready = map(
            sem, ("q_v", "q_ready", "q1_done", "h1_ready", "q2_done", "ys_ready", "t1_ready"))

        part_ready = [sem(f"part_ready{l}") for l in range(2)]
        stack_v = [sem(f"stack_v{l}") for l in range(2)]
        stack_a = [sem(f"stack_a{l}") for l in range(2)]
        v_dup = sem("v_dup")
        lconv_done = [sem(f"lconv_done{l}") for l in range(2)]
        yb_ready, keep_ready, o_ready, last_ready = map(
            sem, ("yb_ready", "keep_ready", "o_ready", "last_ready"))

        block = ctx.enter_context(nc.Block())

        def wait(eng, s, n):
            if not (isinstance(n, int) and n <= 0):
                eng.wait_ge(s, n)

        def inner(t, r0=0, rows=H):
            return t[:, 1 + r0:1 + r0 + rows, 1:1 + W]

        def by_rows(t, odd):
            return t.rearrange("p (t k w) -> p t k w", t=TR, k=2)[:, :, odd, :]

        def img(t, rows=H):
            return t.rearrange("p (h w) -> p h w", h=rows)

        SUMS, SB = 0, 3
        DEL, NDEL = 9, 12
        PART1, PART2 = 15, 21
        AL, TMP = 27, 30
        GM, RS = 36, 38
        SW, RSW = 50, 52
        PQ = 66
        PWR, IPW = 54, 56
        KK, KP, AA, CUTS = 58, 70, 64, 72
        BD = 60
        PC = 68
        SIG = 44
        BSC, BSH = 0, 1
        BT = 2
        MW1, MW2, MC, MD, MI2, MH2, MIC, MHC = range(8)

        @block.sync
        def _(sp):
            sp.dma_start(xin[:, 0, :], x[:, 0, :]).then_inc(s_x[0], 16)
            for k in range(3):
                dy = slice(3 * HID * k, 3 * HID * k + 3 * HID)
                sp.dma_start(w2ar[:, dy], w2a[:, dy]).then_inc(s_w2a[k], 16)
            for c in range(1, NCH):
                sp.dma_start(xin[:, c, :], x[:, c, :]).then_inc(s_x[c], 16)
            sp.dma_start(w3r[:, 0, :], w3[0:P]).then_inc(s_w3, 16)
            sp.dma_start(w3r[0:HB, 1, :], w3[P:HID]).then_inc(s_w3, 16)
            sp.dma_start(w3r[HB:P, 1, :], w3[P:HID]).then_inc(s_w3, 16)

            def spread(c):
                sp.wait_ge(x_split, c + 1)
                for g in range(0 if c else 1, G):
                    for k in range(3):
                        arrived = s_ximg1 if (c, g) == (0, 1) else s_xk[c]
                        sp.dma_start(xk[C * k:C * k + C, G * c + g, :],
                                     xpart[C * g:C * g + C, c % 2, k, :]).then_inc(arrived, 16)

            spread(0)
            for g in range(G):
                q = slice(C * g, C * g + C)
                for k, w in enumerate((wq1, wq2)):
                    sp.dma_start(wqr[q, k, :], w).then_inc(s_wq, 16)
                for k, w in enumerate((wc, wd)):
                    sp.dma_start(wcr[q, k, :], w).then_inc(s_wc, 16)
            for c in range(1, NCH):
                spread(c)

            def dup(layer, c):
                if (layer, c) in V_DUP:
                    return
                sp.wait_ge(stack_v[layer], c + 1)
                sp.wait_ge(stack_a[layer], c + 1)
                flat = "p g h w -> p (g h w)"
                sp.dma_start(kst[2 * C:P, layer, c % 2].rearrange(flat),
                             kst[0:2 * C, layer, c % 2].rearrange(flat)).then_inc(s_dup[layer][c], 16)

            for kind, c in TAIL:
                if kind == "q":
                    dup(0, c)
                elif kind == "c":
                    dup(1, c)
                else:
                    pieces = 1 if c < NCH - 1 else 2
                    for h in range(pieces):
                        px = slice(HW // pieces * h, HW // pieces * (h + 1))
                        sp.wait_ge(*((o_ready, c + 1) if pieces == 1 else (last_ready, h + 1)))
                        sp.dma_start(out[:, c, px], om[:, c, px]).then_inc(s_out, 16)
            sp.wait_ge(s_out, 16 * (NCH + 1))

        @block.gpsimd
        def _(pool):
            nc.gpsimd.memset(col[:], 0.0).then_inc(pool_zeroed, 1)
            nc.gpsimd.memset(ones[:], 1.0).then_inc(pool_zeroed, 1)

            n = [0]

            def link(ins):
                n[0] += 1
                ins.then_inc(pool_chain, 1)
                pool.wait_ge(pool_chain, n[0])

            pts = nc.gpsimd.tensor_scalar

            def cast(out_, in_):
                return pts(out_, in_, 1.0, 1.0, ALU.mult, ALU.mult)

            def split(c):
                pool.wait_ge(s_x[c], 16)
                if c >= 2:
                    pool.wait_ge(s_ximg1, 48)
                    pool.wait_ge(s_xk[c - 2], XK[c - 2])
                b = [xpart[:, c % 2, k, :] for k in range(3)]
                r = [xrest[:, 0, :], xrest[:, 1, :]]
                link(cast(b[0], xin[:, c, :]))
                link(nc.gpsimd.tensor_tensor(r[0], xin[:, c, :], b[0], ALU.subtract))
                link(cast(b[1], r[0]))
                link(nc.gpsimd.tensor_tensor(r[1], r[0], b[1], ALU.subtract))
                cast(b[2], r[1]).then_inc(x_split, 1)

            link(nc.gpsimd.memset(magic[:, 0:1], -MAGIC))
            nc.gpsimd.memset(magic[:, 1:2], MAGIC).then_inc(pool_zeroed, 1)
            nc.gpsimd.memset(expo[:], -0.5).then_inc(pool_zeroed, 1)
            nc.gpsimd.memset(hp[:], 0.0).then_inc(pool_zeroed, 1)

            pool.wait_ge(s_par, 16)
            pool.wait_ge(pool_zeroed, 4)
            kind = [par[:, NBN * k:NBN * k + NBN] for k in range(4)]
            link(nc.gpsimd.tensor_scalar(bn[:, BT, :], kind[KV], EPS, None, ALU.add))
            link(nc.gpsimd.tensor_tensor(bn[:, BT + 1, :], bn[:, BT, :], expo[:], ALU.pow))
            link(nc.gpsimd.tensor_tensor(bn[:, BSC, :], bn[:, BT + 1, :], kind[KG], ALU.mult))
            link(nc.gpsimd.tensor_tensor(kind[KM][:, BNC:BND + 1], kind[KM][:, BNC:BND + 1],
                                         par[:, 4 * NBN:4 * NBN + 2], ALU.subtract))
            link(nc.gpsimd.tensor_tensor(bn[:, BT, :], kind[KM], bn[:, BSC, :], ALU.mult))
            link(nc.gpsimd.tensor_tensor(bn[:, BSH, :], kind[KB], bn[:, BT, :], ALU.subtract))
            nc.gpsimd.tensor_scalar(bn[:, BSH, BN1A:BN3], bn[:, BSH, BN1A:BN3], S0, None,
                                    ALU.mult).then_inc(inv_ready, 1)
            for b in range(2):
                nc.gpsimd.memset(hb[:, b], 0.0).then_inc(pool_zeroed, 1)
            link(nc.gpsimd.memset(ident[:], 0.0))
            nc.gpsimd.affine_select(out=ident[:], in_=ident[:], compare_op=ALU.not_equal, fill=1.0, base=0,
                                    pattern=[[-1, P]], channel_multiplier=1).then_inc(pool_ident, 1)
            pool.wait_ge(x0_ready, 1)
            for c in range(1, NCH):
                split(c)
            for t in (qi[:].rearrange("p c h w -> p (c h w)"), wqi[:].rearrange("p k t o -> p (k t o)"),
                      part[:, 0].rearrange("p b k h w -> p (b k h w)")):
                nc.gpsimd.memset(t.bitcast(F32), 0.0).then_inc(pool_zeroed, 1)
            pool.wait_ge(hb_ready, B)
            nc.gpsimd.memset(part[:, 1], 0.0).then_inc(pool_zeroed, 1)

            for c in range(NCH - 1):
                at = LTAIL.index(("d", c))
                pool.wait_ge(keep_ready, at + 1)
                pts(om[:, c, :], yb[:, at % 2, :], keep[:, at:at + 1], 1.0, ALU.mult, ALU.mult).then_inc(o_ready, 1)

        @block.tensor
        def _(pe):
            pe.wait_ge(pool_zeroed, 2)

            def total(n, w, *cols):
                for k, c in enumerate(cols):
                    i = nc.tensor.matmul(ps[:, TOTAL_BANK[n], 8 * n:8 * n + w], ones[:], c, start=(k == 0),
                                         stop=(k == len(cols) - 1))
                i.then_inc(sums_done, 1)

            pe.wait_ge(sums_ready, 1)
            total(1, 1, col[:, SUMS:SUMS + 1])

            def keep_warm(n, bank):
                for _ in range(n):
                    nc.tensor.matmul(ps[:, bank, :HALF], w2at[:, 0, 0:P], vh[:, 0, 0, 0, 0:HALF_ROWS, 0:W],
                                     start=True, stop=True)

            def expand(j, n, bank=6):
                two, h = divmod(n, 2)
                if n == 0:
                    if isinstance(j, int) and j == 1:
                        pe.wait_ge(s_ximg1, 48)
                    if isinstance(j, int) and j in (2, G):
                        pe.wait_ge(s_xk[j // G], XK[j // G])
                    wait(pe, rb_ready, 2 * j)
                elif bank == 6:
                    pe.wait_ge(*((ra_ready, 2 * j + n) if n < 3 else (rb_ready, 2 * j + 1)))
                nc.tensor.matmul(ps[:, bank, :HALF], (w1t[:, 0:P], w1t[:, P:P + 2 * HB])[two],
                                 xk[:, j, HALF * h:HALF * h + HALF],
                                 start=True, stop=True).then_inc((expa_done, expb_done)[two], 1)

            def weights(k, dx, rest):
                o = slice(P, HID) if rest else slice(0, P)
                if k in (0, 3):
                    return w2at[:, 2 * k + dx, o]
                return wun[:, dx, :] if rest and k == 2 else wu[:, k - 1, dx, o]

            def rows(b, odd, t):
                dy, dx = divmod(t, 3)
                r0 = dy + odd
                return hb[:, b, r0:r0 + 2 * TR - 1:2, dx:dx + W]

            def product(k, b, parts=(0, 1), plain=True):
                last = k in (1, 2)
                for part in parts:
                    for dx in range(3):
                        i = nc.tensor.matmul(ps[:, k, :HALF], weights(k, dx, False),
                                             vh[:, b, part, k, :, dx:dx + W], start=(part == 0 and dx == 0),
                                             stop=(last and part == 1 and dx == 2))
                if plain and not last:
                    for t in range(TAPS):
                        i = nc.tensor.matmul(ps[:, k, :HALF], w2bt[:, t, 0:P], rows(b, k // 3, t), start=False,
                                             stop=(t == TAPS - 1))
                if last or plain:
                    i.then_inc(m_done, 1)

            def pair(bank, ks, b):
                plain = bank == 5
                for part in range(2):
                    for dx in range(3):
                        for q, k in enumerate(ks):
                            i = nc.tensor.matmul(ps[HB * q:HB * q + HB, bank, :HALF], weights(k, dx, True),
                                                 vh[:, b, part, k, :, dx:dx + W], start=(part == 0 and dx == 0),
                                                 stop=(not plain and part == 1 and dx == 2))
                if plain:
                    for t in range(TAPS):
                        for q in range(2):
                            i = nc.tensor.matmul(ps[HB * q:HB * q + HB, bank, :HALF], w2bt[:, t, P:HID],
                                                 rows(b, q, t), start=False, stop=(t == TAPS - 1))
                    i.then_inc(convb_done, 1)

            def project(c, h, steps=(0, 1, 2, 3), bank=7):
                wait(pe, y0_ready, 2 * c + h if bank == 7 else 0)
                lower = slice(HB * h, HB * h + HB)
                for s in steps:
                    if s < 2:
                        pe.wait_ge((h2a_ready, h2_ready)[s], (c + 1) * G)
                    for g in range(G):
                        w, rhs = ((w3t[:, 0, :], by_rows(h2a[:, g, s, :], h)) if s < 2 else
                                  (w3t[lower, 1, :], h2b[lower, g, s - 2, :]))
                        i = nc.tensor.matmul(ps[C * g:C * g + C, bank, :HALF], w, rhs, start=(s == 0), stop=(s == 3))
                if 3 in steps:
                    i.then_inc(proj_done, 1)

            def slot(c, g, first=False, last=False):
                j = c * G + g
                b = g % 2
                ahead = not last or g < G - 2
                if first and g == 0:
                    pe.wait_ge(w2_ready, 1)
                    pe.wait_ge(vhi_ready, 1)
                    product(0, b, parts=(0,), plain=False)
                    product(3, b, parts=(0,), plain=False)
                    expand(j + 2, 0)
                    pe.wait_ge(va_ready, 1)
                    product(0, b, parts=(1,), plain=False)
                    product(3, b, parts=(1,), plain=False)
                    pe.wait_ge(w2_ready, 2)
                    product(1, b)
                    product(2, b)
                    expand(j + 2, 1)
                    pe.wait_ge(w2_ready, 3)
                    pe.wait_ge(hb_ready, 1)
                    product(0, b, parts=())
                    expand(j + 2, 2)
                    product(3, b, parts=())
                    expand(j + 2, 3)
                else:
                    if ahead:
                        expand(j + 2, 0)
                    pe.wait_ge(va_ready, j + 1)
                    pe.wait_ge(c1_ready, j)
                    product(1, b)
                    pe.wait_ge(out_v, 3 * j - 2)
                    product(2, b)
                    if ahead:
                        expand(j + 2, 1)
                    pe.wait_ge(out_v, 3 * j - 1)
                    pe.wait_ge(hb_ready, j + 1)
                    product(0, b)
                    if ahead:
                        expand(j + 2, 2)
                    if g == 0 and not first:
                        if not isinstance(c, int):
                            pe.wait_ge(w3_ready, 1)
                        project(c - 1, 0)
                    pe.wait_ge(out_v, 3 * j)
                    product(3, b)
                    if ahead:
                        expand(j + 2, 3)
                    pe.wait_ge(z_ready, j)
                pair(4, (1, 2), b)
                if g == 0 and not first:
                    project(c - 1, 1)
                pair(5, (0, 3), b)
                if first and g == 0:
                    pe.wait_ge(sums_ready, 3)
                    pe.wait_ge(a_sum, 5)
                    total(4, 6, col[:, PART1:PART1 + 6], col[:, PART2:PART2 + 6])

            pe.wait_ge(sums_ready, 2)
            total(2, 2, col[:, PART1:PART1 + 4:3])
            pe.wait_ge(a_sum, 1)
            total(3, 1, col[:, SUMS + 1:SUMS + 2], col[:, SB + 1:SB + 2])
            pe.wait_ge(w1_ready, 1)
            pe.wait_ge(x0_ready, 1)
            for n in range(4):
                expand(0, n, bank=n)
            pe.wait_ge(w3s_ready, 1)
            pe.wait_ge(thr_ready, 1)
            total(5, 1, col[:, SUMS + 2:SUMS + 3], col[:, SB + 2:SB + 3])
            for n in range(4):
                expand(1, n)
            slot(0, 0, first=True)
            slot(0, 1, first=True)
            pe.wait_ge(pool_ident, 1)
            pe.wait_ge(mxt_go, 1)
            nc.tensor.transpose(ps[0:8, 7, P:2 * P], mx[:, 0:8], ident[:]).then_inc(mxt_done, 1)
            slot(0, 2, first=True)
            pe.wait_ge(mxt_go, 2)
            nc.tensor.matmul(ps[:, 7, 64:72], ones[0:8, :], diag[0:8, :], start=True, stop=True).then_inc(mxt_done, 1)
            slot(0, 3, first=True)
            for c in range(2, NCH):
                pe.wait_ge(s_xk[c], XK[c])
            with pe.Fori(1, NCH - 1) as c:
                for g in range(G):
                    slot(c, g)
            for g in range(G):
                slot(NCH - 1, g, last=True)
            pe.wait_ge(rb_ready, 2 * B)
            keep_warm(16, 6)
            project(NCH - 1, 0, (0,))
            project(NCH - 1, 1, (0,), bank=6)
            project(NCH - 1, 0, (1, 2, 3))
            project(NCH - 1, 1, (1, 2, 3), bank=6)

            def largest(n):
                pe.wait_ge(gm_go, 2 * n + 1)
                nc.tensor.transpose(ps[0:1, 5, 0:P], mx[:, 8:9], ident[:]).then_inc(gm_done, 1)
                pe.wait_ge(gm_go, 2 * n + 2)
                nc.tensor.matmul(ps[:, 5, 0:1], ones[0:1, :], rowm[0:1, 0:1], start=True,
                                 stop=True).then_inc(gm_done, 1)

            def qconv(k, c, bank, done):
                for h in range(2):
                    pe.wait_ge(q_ready, 2 * (NCH * k + c) + h + 1)
                    for t in range(TAPS):
                        dy, dx = divmod(t, 3)
                        r0 = HALF_ROWS * h + dy
                        i = nc.tensor.matmul(ps[:, bank + h, :HALF], wqi[:, k, t, :],
                                             qi[:, c, r0:r0 + HALF_ROWS, dx:dx + W],
                                             start=(t == 0), stop=(t == TAPS - 1))
                    i.then_inc(done, 1)

            keep_warm(8, 4)
            pe.wait_ge(wl_ready, 2)
            largest(0)
            keep_warm(10, 4)
            for c in range(NCH):
                wait(pe, h1_ready, 2 * (c - 1))
                qconv(0, c, 2 * (c % 2), q1_done)
            keep_warm(8, 4)
            largest(1)
            keep_warm(10, 4)

            def lconv(layer, c):
                if c == 0:
                    pe.wait_ge(wst_ready, layer + 1)
                if (layer, c) in V_DUP:
                    pe.wait_ge(v_dup, V_DUP.index((layer, c)) + 1)
                else:
                    pe.wait_ge(s_dup[layer][c], 16)
                bank = 2 + 2 * layer
                wait(pe, yb_ready, 2 * DONE_BEFORE["cd"[layer], c])
                for h in range(2):
                    for t in range(TAPS):
                        dy, dx = divmod(t, 3)
                        r0 = HALF_ROWS * h + dy
                        for g in range(G):
                            i = nc.tensor.matmul(ps[C * g:C * g + C, bank + h, :HALF],
                                                 wst[:, layer, C * t:C * t + C],
                                                 kst[:, layer, c % 2, g, r0:r0 + HALF_ROWS, dx:dx + W],
                                                 start=(t == 0), stop=(t == TAPS - 1))
                    i.then_inc(lconv_done[layer], 1)

            for kind, c in TAIL:
                if kind == "q":
                    wait(pe, t1_ready, c - 1)
                    qconv(1, c, QBANK[c % 2], q2_done)
                else:
                    lconv("cd".index(kind), c)

        @block.scalar
        def _(act):
            act.dma_start(w1r[:], w1).then_inc(s_w1, 16)
            act.dma_start(w2br[0:HB, :], w2b).then_inc(s_w2b, 16)
            act.dma_start(par[:], params).then_inc(s_par, 16)
            n = [0]

            def link(ins):
                n[0] += 1
                ins.then_inc(a_chain, 1)
                act.wait_ge(a_chain, n[0])

            act.wait_ge(pool_zeroed, 2)
            for k in range(3):
                dy = slice(3 * HID * k, 3 * HID * k + 3 * HID)
                act.wait_ge(s_w2a[k], 16)
                nc.scalar.activation(ajunk[:, dy], w2ar[:, dy], ACT.Abs,
                                     accum_out=cm[:, 0, 0:3, 1][:, k:k + 1]).then_inc(a_abs, 1)
            act.wait_ge(s_w2b, 16)
            link(nc.scalar.activation(wjunk[0:HB, :], w2br[0:HB, :], ACT.Abs,
                                      accum_out=col[0:HB, SB + 1:SB + 2]))
            act.wait_ge(a_abs, 3)
            nc.scalar.activation(cm[:, 1, 0:3, 1], cm[:, 0, 0:3, 1], ACT.Copy,
                                 accum_out=col[:, SUMS + 1:SUMS + 2]).then_inc(a_sum, 1)

            def relu_exp(j, n, b, bank=6):
                two, h = divmod(n, 2)
                done, ready, at = ((expa_done, ra_ready, BN1A), (expb_done, rb_ready, BN1B))[two]
                dst = raj[b][:, two, :]
                act.wait_ge(done, 2 * j + h + 1)
                if h == 0:
                    wait(act, (hp_done, hb_ready)[two], j - 1)
                nc.scalar.activation(dst[:, HALF * h:HALF * h + HALF], ps[:, bank, :HALF], ACT.Relu,
                                     bias=bn[:, BSH, at:at + 1], scale=bn[:, BSC, at:at + 1]).then_inc(ready, 1)

            def copy_m1(j):
                act.wait_ge(m_done, 4 * j + 1)
                wait(act, out_v, 3 * j - 2)
                nc.scalar.copy(c1a[:], ps[:, 1, :HALF]).then_inc(c1_ready, 1)

            def copy_y(j):
                act.wait_ge(convb_done, j + 1)
                wait(act, z_half, j)
                nc.scalar.mul(cy[0:HB, :], ps[HB:P, 4, :HALF], -1.0)
                nc.scalar.copy(cy[HB:P, :], ps[0:HB, 4, :HALF]).then_inc(cy_ready, 1)

            def hi(j, b):
                act.wait_ge(v_ready, j + 1)
                wait(act, convb_done, j - 1)
                nc.scalar.copy(vh[:, b, 0].rearrange("p k h w -> p (k h w)"),
                               va[:].rearrange("p k h w -> p (k h w)")).then_inc(vhi_ready, 1)

            def relu_a(j):
                act.wait_ge(out_v, 3 * j + 3)
                nc.scalar.activation(r2a[:], r2a[:], ACT.Relu, bias=bn[:, BSH, BN2A:BN2A + 1],
                                     scale=bn[:, BSC, BN2A:BN2A + 1]).then_inc(r2a_ready, 1)

            def relu_b(j):
                act.wait_ge(z_ready, j + 1)
                nc.scalar.activation(r2b[:], r2b[:], ACT.Relu, bias=bn[:, BSH, BN2B:BN2B + 1],
                                     scale=bn[:, BSC, BN2B:BN2B + 1]).then_inc(r2b_ready, 1)

            def add_shift(c):
                if isinstance(c, int) and c == 0:
                    act.wait_ge(bn_ready, 1)
                act.wait_ge(x_split, c + 1)
                nc.scalar.activation(xin[:, c, :], xin[:, c, :], ACT.Identity,
                                     bias=bn[:, BSH, BN3:BN3 + 1]).then_inc(xs_ready, 1)

            def slot(c, g, first=False, last=False):
                j = c * G + g
                begin = first and g == 0
                end = last and g == G - 1
                ahead = not last or g < G - 2
                if not begin:
                    copy_y(j - 1)
                if ahead:
                    relu_exp(j + 2, 0, g % 2)
                if not begin:
                    relu_b(j - 1)
                copy_m1(j)
                if ahead:
                    relu_exp(j + 2, 1, g % 2)
                if not end:
                    hi(j + 1, (g + 1) % 2)
                if ahead:
                    relu_exp(j + 2, 2, g % 2)
                    relu_exp(j + 2, 3, g % 2)
                if begin:
                    act.wait_ge(w2_ready, 3)
                    nc.scalar.activation(ajunk, w2at[:].rearrange("p t o -> p (t o)"), ACT.Square,
                                         accum_out=col[:, PART1 + 4:PART1 + 5]).then_inc(a_sum, 1)
                    nc.scalar.activation(wjunk[0:HB, :], w2bt[0:HB].rearrange("p t o -> p (t o)"), ACT.Square,
                                         accum_out=col[0:HB, PART2 + 4:PART2 + 5]).then_inc(a_sum, 1)
                    act.wait_ge(bn_ready, 1)
                relu_a(j)
                if g == 1:
                    add_shift(c)

            act.wait_ge(thr_ready, 1)
            nc.scalar.activation(ajunk, ajunk, ACT.Relu, bias=col[:, NDEL + 1:NDEL + 2],
                                 accum_out=col[:, PART1 + 1:PART1 + 2]).then_inc(a_sum, 1)
            act.wait_ge(bn1_ready, 1)
            for quarter in range(4):
                relu_exp(0, quarter, 0, bank=quarter)
            nc.scalar.activation(wjunk[0:HB, :], wjunk[0:HB, :], ACT.Relu, bias=col[0:HB, NDEL + 1:NDEL + 2],
                                 accum_out=col[0:HB, PART2 + 1:PART2 + 2]).then_inc(a_sum, 1)
            act.wait_ge(a_sum, 3)
            hi(0, 0)
            for quarter in range(4):
                relu_exp(1, quarter, 1)

            def integers(k):
                link(nc.scalar.activation(wqq[:, k, :], wqr[:, k, :], ACT.Identity, bias=magic[:, 1:2],
                                          scale=col[:, RSW + k:RSW + k + 1]))
                for g in range(G):
                    q = slice(C * g, C * g + C)
                    i = nc.scalar.activation(wqi[q, k, :, C * g:C * g + C],
                                             wqq[q, k, :].rearrange("p (t o) -> p t o", t=TAPS),
                                             ACT.Identity, bias=magic[q, 0:1])
                i.then_inc(wl_ready, 1)

            for g in range(G):
                slot(0, g, first=True)
            act.wait_ge(ws_ready, 1)
            act.wait_ge(pool_zeroed, 10)
            with act.Fori(1, NCH - 1) as c:
                for g in range(G):
                    slot(c, g)
            for g in range(G):
                slot(NCH - 1, g, last=True)
                if g < 2:
                    integers(g)
            copy_y(B - 1)
            relu_b(B - 1)

            ROWS = (slice(0, HALF_ROWS + 1), slice(HALF_ROWS + 1, H))

            def quant(c, k):
                for h, rows in enumerate(ROWS):
                    act.wait_ge(q_v, 2 * (NCH * k + c) + h + 1)
                    nc.scalar.activation(inner(qi[:, c])[:, rows], img(qf[:, c % 2, :])[:, rows], ACT.Relu,
                                         bias=magic[:, 0:1]).then_inc(q_ready, 1)

            def out1(c):
                for h in range(2):
                    act.wait_ge(q1_done, 2 * c + h + 1)
                    nc.scalar.activation(h1[:, c, HALF * h:HALF * h + HALF], ps[:, 2 * (c % 2) + h, :HALF], ACT.Relu,
                                         bias=bn[:, BSH, BNQ1:BNQ1 + 1],
                                         scale=col[:, SIG:SIG + 1]).then_inc(h1_ready, 1)

            act.wait_ge(pool_zeroed, 10)
            quant(0, 0)
            act.wait_ge(scale_ready, 1)
            for c in range(1, NCH):
                quant(c, 0)
                out1(c - 1)
            out1(NCH - 1)
            act.wait_ge(q1_done, 2 * NCH)
            for c in range(2):
                quant(c, 1)
            act.wait_ge(scale_ready, 2)
            for c in range(NCH):
                if c >= 2:
                    quant(c, 1)
                nc.scalar.activation(y0[:, c, :], y0[:, c, :], ACT.Identity, bias=col[:, SIG + 3:SIG + 4],
                                     scale=col[:, BD + 2:BD + 3]).then_inc(ys_ready, 1)

            def stack(layer, c):
                act.wait_ge(part_ready[layer], 2 * c + 2)
                wait(act, lconv_done[layer], 2 * (c - 1))
                if layer == 1:
                    n = LTAIL.index(("c", c))
                    act.wait_ge(keep_ready, n + 1)
                for g, k in A_SHARE:
                    q = slice(C * g, C * g + C)
                    dst, src = kst[C * k:C * k + C, layer, c % 2, g], part[q, layer, c % 2, k]
                    if layer == 0:
                        ins = nc.scalar.copy(dst, src)
                    else:
                        ins = nc.scalar.mul(dst, src, keep[q, n:n + 1])
                ins.then_inc(stack_a[layer], 1)

            def relu_l(layer, c):
                k = BNC + layer
                n = LTAIL.index(("cd"[layer], c))
                if n >= 2:
                    k2, c2 = LTAIL[n - 2]
                    act.wait_ge(*((part_ready[1], 2 * c2 + 2) if k2 == "c" else (o_ready, c2 + 1)))
                for h in range(2):
                    act.wait_ge(lconv_done[layer], 2 * c + h + 1)
                    nc.scalar.activation(yb[:, n % 2, HALF * h:HALF * h + HALF], ps[:, 2 + 2 * layer + h, :HALF],
                                         ACT.Relu, bias=bn[:, BSH, k:k + 1],
                                         scale=col[:, SIG + 4 + layer:SIG + 5 + layer]).then_inc(yb_ready, 1)

            for kind, c in TAIL:
                if kind == "q":
                    stack(0, c)
                else:
                    relu_l("cd".index(kind), c)
                    if kind == "c":
                        stack(1, c)

        @block.vector
        def _(dve):
            n = [0]

            def link(ins):
                n[0] += 1
                ins.then_inc(v_chain, 1)
                dve.wait_ge(v_chain, n[0])

            def c1(k, p=P, w=1):
                return col[0:p, k:k + w]

            ts, tt, stt = nc.vector.tensor_scalar, nc.vector.tensor_tensor, nc.vector.scalar_tensor_tensor

            def ternary(raw, out_, neg, k, p):
                link(ts(neg, raw, c1(NDEL + k, p), None, ALU.is_lt))
                return stt(out_, raw, c1(DEL + k, p), neg, ALU.is_gt, ALU.subtract)

            def threshold(k, n, count):
                link(ts(c1(DEL + k), ps[:, TOTAL_BANK[n], 8 * n:8 * n + 1], 1.0 / count, 0.7, ALU.mult, ALU.mult))
                link(ts(c1(NDEL + k), c1(DEL + k), -1.0, None, ALU.mult))

            def alpha1():
                wt, t2 = (ps[:, TOTAL_BANK[2], 16 + k:17 + k] for k in range(2))
                link(ts(c1(TMP), t2, 1.0, None, ALU.max))
                link(nc.vector.reciprocal(c1(TMP), c1(TMP)))
                link(tt(c1(AL), c1(TMP), wt, ALU.mult))

            dve.wait_ge(pool_zeroed, 2)
            dve.wait_ge(s_w1, 16)
            nc.vector.tensor_reduce(c1(SUMS, C), w1r[:], AX.X, ALU.add,
                                    apply_absolute_value=True).then_inc(sums_ready, 1)

            dve.wait_ge(sums_done, 1)
            threshold(0, 1, N1)
            link(ternary(w1r[:], w1t[0:C, 0:HID], wneg[0:C, 0:HID], 0, C))
            link(nc.vector.tensor_copy(w1t[0:C, HID:HID + HB], w1t[0:C, P:HID]))
            for k in (1, 2):
                i = nc.vector.tensor_copy(w1t[C * k:C * k + C, :], w1t[0:C, :])
            i.then_inc(w1_ready, 1)
            stt(r2a[0:C, 0:HID], w1r[:], 1.0, w1t[0:C, 0:HID], ALU.mult, ALU.mult, accum_out=c1(PART1, C))
            stt(r2a[0:C, HID:2 * HID], w1t[0:C, 0:HID], 1.0, w1t[0:C, 0:HID], ALU.mult, ALU.mult,
                accum_out=c1(PART1 + 3, C)).then_inc(sums_ready, 1)
            dve.wait_ge(s_x[0], 16)
            xb = [xpart[:, 0, k, :] for k in range(3)]
            link(nc.vector.tensor_copy(xb[0], xin[:, 0, :]))
            link(tt(xrest[:, 0, :], xin[:, 0, :], xb[0], ALU.subtract))
            link(nc.vector.tensor_copy(xb[1], xrest[:, 0, :]))
            dve.wait_ge(sums_done, 2)
            alpha1()
            dve.wait_ge(inv_ready, 1)
            ts(bn[:, BSC, BN1A:BN2A], bn[:, BSC, BN1A:BN2A], c1(AL), S0, ALU.mult, ALU.mult).then_inc(bn1_ready, 1)
            dve.wait_ge(sums_done, 3)
            link(ts(c1(DEL + 1), ps[:, TOTAL_BANK[3], 24:25], 1.0 / N2, 0.7, ALU.mult, ALU.mult))
            ts(c1(NDEL + 1), c1(DEL + 1), -1.0, None, ALU.mult).then_inc(thr_ready, 1)
            link(tt(xrest[:, 1, :], xrest[:, 0, :], xb[1], ALU.subtract))
            nc.vector.tensor_copy(xb[2], xrest[:, 1, :]).then_inc(x_split, 1)
            dve.wait_ge(x_split, 1)
            for k in range(3):
                i = nc.vector.tensor_copy(xk[C * k:C * k + C, 0, :], xpart[0:C, 0, k, :])
            i.then_inc(x0_ready, 1)

            dve.wait_ge(s_w3, 48)
            nc.vector.tensor_reduce(c1(SUMS + 2), w3r[:, 0, :], AX.X, ALU.add, apply_absolute_value=True)
            nc.vector.tensor_reduce(c1(SB + 2, HB), w3r[0:HB, 1, :], AX.X, ALU.add,
                                    apply_absolute_value=True).then_inc(w3s_ready, 1)
            flat = "p t o -> p (t o)"
            DY = 3 * HID

            def w2_row(k):
                dy = slice(DY * k, DY * k + DY)
                return stt(w2at[:].rearrange(flat)[:, dy], w2ar[:, dy], c1(DEL + 1), wneg[:, dy],
                           ALU.is_gt, ALU.subtract)

            def w2_rows():
                dve.wait_ge(thr_ready, 1)
                link(ts(wneg, w2ar, c1(NDEL + 1), None, ALU.is_lt))
                for k in (0, 2):
                    i = w2_row(k)
                i.then_inc(w2_ready, 1)

            def w2_transforms():
                link(w2_row(1))
                t = w2at[:].rearrange(flat)
                u = wu[:].rearrange("p k d o -> p k (d o)")
                g = [t[:, DY * k:DY * k + DY] for k in range(3)]
                link(tt(wneg[:, 0:DY], g[0], g[2], ALU.add))
                tt(u[:, 0], wneg[:, 0:DY], g[1], ALU.add)
                link(tt(u[:, 1], wneg[:, 0:DY], g[1], ALU.subtract))
                both = wu[:].rearrange("p k d o -> p (k d o)")
                link(ts(both, both, 0.5, None, ALU.mult))
                ts(wun[:], wu[:, 1, :, P:HID], -1.0, None, ALU.mult).then_inc(w2_ready, 1)

            def w2_rest():
                t = w2bt[:].rearrange(flat)
                dve.wait_ge(w2_ready, 2)
                link(ternary(w2br[0:HB, :], t[0:HB], wneg[0:HB, :], 1, HB))
                nc.vector.tensor_copy(t[HB:P], t[0:HB]).then_inc(w2_ready, 1)

            def clamp(j, b):
                dve.wait_ge(ra_ready, 2 * j + 2)
                if isinstance(j, int) and j == 0:
                    dve.wait_ge(pool_zeroed, 5)
                ts(inner(hp), img(raj[b][:, 0, :]), CAP, None, ALU.min).then_inc(hp_done, 1)
                dve.wait_ge(hp_done, j + 1)

            def transforms(j):
                wait(dve, vhi_ready, j)
                d = [hp[:, k:k + 2 * TR - 1:2, :] for k in range(4)]
                for k, (x0, x1, op) in enumerate(((0, 2, ALU.subtract), (1, 2, ALU.add), (2, 1, ALU.subtract),
                                                  (3, 1, ALU.subtract))):
                    i = tt(va[:, k], d[x0], d[x1], op)
                i.then_inc(v_ready, 1)

            def lo(j, b):
                dve.wait_ge(vhi_ready, j + 1)
                v = "p k h w -> p (k h w)"
                tt(vh[:, b, 1].rearrange(v), va[:].rearrange(v), vh[:, b, 0].rearrange(v),
                   ALU.subtract).then_inc(va_ready, 1)

            def halves_b(j, b):
                dve.wait_ge(rb_ready, 2 * j + 2)
                wait(dve, convb_done, j - 1)
                if isinstance(j, int) and j == 0:
                    dve.wait_ge(pool_zeroed, 7)
                ts(inner(hb[:, b]), img(raj[b][:, 1, :]), CAP, None, ALU.min).then_inc(hbhi_done, 1)
                dve.wait_ge(hbhi_done, j + 1)
                up = slice(HB, P)
                low = hb[up, b, 1:1 + H, 1:1 + W]
                stt(low, img(raj[b][:, 1, :])[up], CAP, low, ALU.min,
                    ALU.subtract).then_inc(hb_ready, 1)

            def out_12(j):
                dve.wait_ge(c1_ready, j + 1)
                dve.wait_ge(m_done, 4 * j + 2)
                tt(ds[:, 0, :], c1a[:], ps[:, 2, :HALF], ALU.add)
                tt(ds[:, 1, :], c1a[:], ps[:, 2, :HALF], ALU.subtract).then_inc(out_v, 1)

            def out_row(j, odd):
                dve.wait_ge(m_done, 4 * j + 3 + odd)
                dve.wait_ge(out_v, 3 * j + 1)
                tt(by_rows(r2a[:], odd), img(ds[:, odd, :], TR),
                   img(ps[:, 3 * odd, :HALF], TR), ALU.add).then_inc(out_v, 1)

            def out_b(j):
                dve.wait_ge(cy_ready, j + 1)
                tt(r2b[:], cy[:], ps[:, 4, :HALF], ALU.add).then_inc(z_half, 1)
                dve.wait_ge(z_half, j + 1)
                tt(r2b[:], r2b[:], ps[:, 5, :HALF], ALU.add).then_inc(z_ready, 1)

            def halves2_a(j, g):
                dve.wait_ge(r2a_ready, j + 1)
                ts(h2a[:, g, 0, :], r2a[:], CAP, None, ALU.min).then_inc(h2hi_done, 1)
                dve.wait_ge(h2hi_done, 2 * j + 1)
                stt(h2a[:, g, 1, :], r2a[:], CAP, h2a[:, g, 0, :], ALU.min, ALU.subtract).then_inc(h2a_ready, 1)

            def halves2_b(j, g):
                dve.wait_ge(r2b_ready, j + 1)
                ts(h2b[:, g, 0, :], r2b[:], CAP, None, ALU.min).then_inc(h2hi_done, 1)
                dve.wait_ge(h2hi_done, 2 * j + 2)
                stt(h2b[:, g, 1, :], r2b[:], CAP, h2b[:, g, 0, :], ALU.min, ALU.subtract).then_inc(h2_ready, 1)

            def residual(c, h, bank=7):
                dve.wait_ge(proj_done, 2 * c + h + 1)
                dve.wait_ge(xs_ready, c + 1)
                rows = by_rows(y0[:, c, :], h)
                stt(rows, img(ps[:, bank, :HALF], TR), bn[:, BSC, BN3:BN3 + 1], by_rows(xin[:, c, :], h),
                    ALU.mult, ALU.add).then_inc(y0_ready, 1)
                dve.wait_ge(y0_ready, 2 * c + h + 1)
                nc.vector.tensor_reduce(cm[:, 0, c, h:h + 1], rows, AX.XY, ALU.max).then_inc(cmax_done, 1)

            def slot(c, g, first=False, last=False):
                j = c * G + g
                begin = first and g == 0
                end = last and g == G - 1
                if not end:
                    clamp(j + 1, (g + 1) % 2)
                    transforms(j + 1)
                if not begin:
                    out_b(j - 1)
                    if g == 1:
                        wait(dve, proj_done, 2 * c)
                    halves2_a(j - 1, (g - 1) % G)
                    out_12(j)
                    halves2_b(j - 1, (g - 1) % G)
                else:
                    out_12(j)
                    w3_rest()
                if not end:
                    lo(j + 1, (g + 1) % 2)
                out_row(j, 0)
                if g == 0 and not first:
                    residual(c - 1, 0)
                if not end:
                    halves_b(j + 1, (g + 1) % 2)
                out_row(j, 1)
                if begin:
                    scales()
                if g == 0 and not first:
                    residual(c - 1, 1)

            def w3_rest():
                dve.wait_ge(sums_done, 4)
                threshold(2, 5, N3)
                ternary(w3r[:].rearrange("p k o -> p (k o)"), w3t[:].rearrange("p k o -> p (k o)"),
                        wneg[:, 0:2 * C], 2, P).then_inc(w3_ready, 1)
                dve.wait_ge(w3_ready, 1)
                junk = r2b[:]
                stt(junk[:, 0:C], w3r[:, 0, :], 1.0, w3t[:, 0, :], ALU.mult, ALU.mult, accum_out=c1(PART1 + 2))
                stt(junk[:, C:2 * C], w3t[:, 0, :], 1.0, w3t[:, 0, :], ALU.mult, ALU.mult, accum_out=c1(PART1 + 5))
                stt(junk[0:HB, 2 * C:3 * C], w3r[0:HB, 1, :], 1.0, w3t[0:HB, 1, :], ALU.mult, ALU.mult,
                    accum_out=c1(PART2 + 2, HB))
                stt(junk[0:HB, 3 * C:4 * C], w3t[0:HB, 1, :], 1.0, w3t[0:HB, 1, :], ALU.mult, ALU.mult,
                    accum_out=c1(PART2 + 5, HB)).then_inc(sums_ready, 1)

            def scales():
                dve.wait_ge(sums_done, 5)
                link(tt(c1(TMP), ps[:, 7, 36:37], c1(DEL + 1), ALU.mult))
                link(tt(c1(TMP + 2), c1(TMP), ps[:, 7, 33:34], ALU.add))
                link(nc.vector.tensor_copy(c1(TMP + 3), ps[:, 7, 34:35]))
                link(ts(c1(TMP, w=2), ps[:, 7, 36:38], 1.0, None, ALU.max))
                link(nc.vector.reciprocal(c1(TMP, w=2), c1(TMP, w=2)))
                link(tt(c1(AL + 1, w=2), c1(TMP, w=2), c1(TMP + 2, w=2), ALU.mult))
                link(ts(bn[:, BSC, BN2A:BN3], bn[:, BSC, BN2A:BN3], c1(AL + 1), None, ALU.mult))
                ts(bn[:, BSC, BN3:BN3 + 1], bn[:, BSC, BN3:BN3 + 1], c1(AL + 2), 1.0 / S0, ALU.mult,
                   ALU.mult).then_inc(bn_ready, 1)

            w2_rows()
            clamp(0, 0)
            transforms(0)
            w2_transforms()
            lo(0, 0)
            w2_rest()
            halves_b(0, 0)
            slot(0, 0, first=True)

            dve.wait_ge(s_wq, 16 * 2 * G)
            dve.wait_ge(s_wc, 16 * 2 * G)
            red = nc.vector.tensor_reduce
            for k in range(2):
                red(mx[:, MW1 + k:MW1 + k + 1], wqr[:, k, :], AX.X, ALU.max, apply_absolute_value=True)
                red(mx[:, MC + k:MC + k + 1], wcr[:, k, :], AX.X, ALU.max, apply_absolute_value=True)
            for m, kk, col_ in ((MI2, BSC, BNQ2), (MH2, BSH, BNQ2), (MIC, BSC, BNC), (MHC, BSH, BNC)):
                i = red(mx[:, m:m + 1], bn[:, kk, col_:col_ + 1], AX.X, ALU.max, apply_absolute_value=True)
            i.then_inc(mxt_go, 1)
            slot(0, 1, first=True)
            dve.wait_ge(mxt_done, 1)
            link(red(rowm[0:8, 1:2], ps[0:8, 7, P:2 * P], AX.X, ALU.max))
            dve.wait_ge(pool_ident, 1)
            ts(diag[0:8, :], ident[0:8, 0:8], rowm[0:8, 1:2], None, ALU.mult).then_inc(mxt_go, 1)
            slot(0, 2, first=True)
            dve.wait_ge(mxt_done, 2)
            link(nc.vector.tensor_copy(mxa[:], ps[:, 7, 64:72]))
            link(ts(c1(SW, w=2), mxa[:, MW1:MW1 + 2], 1e-8, 1.0 / WQ, ALU.max, ALU.mult))
            link(nc.vector.reciprocal(c1(RSW, w=2), c1(SW, w=2)))
            link(ts(c1(PWR, w=2), mxa[:, MC:MC + 2], 1e-30, None, ALU.max))
            link(ts(c1(PWR, w=2).bitcast(I32), c1(PWR, w=2).bitcast(I32), 0x7F800000, None, ALU.bitwise_and))
            nc.vector.reciprocal(c1(IPW, w=2), c1(PWR, w=2)).then_inc(ws_ready, 1)
            slot(0, 3, first=True)

            with dve.Fori(1, NCH - 1) as c:
                for g in range(G):
                    slot(c, g)
            for g in range(G):
                slot(NCH - 1, g, last=True)
            halves2_a(B - 1, G - 1)
            out_b(B - 1)
            halves2_b(B - 1, G - 1)
            residual(NCH - 1, 0)
            residual(NCH - 1, 1, bank=6)

            def step(k):
                dve.wait_ge(cmax_done, 2 * NCH * (k + 1))
                red(mx[:, 8:9], cm[:, k].rearrange("p c h -> p (c h)"), AX.X, ALU.max).then_inc(gm_go, 1)
                dve.wait_ge(gm_done, 2 * k + 1)
                red(rowm[0:1, 0:1], ps[0:1, 5, 0:P], AX.X, ALU.max).then_inc(gm_go, 1)
                dve.wait_ge(gm_done, 2 * k + 2)
                link(ts(c1(GM + k), ps[:, 5, 0:1], 1e-8, None, ALU.max))
                link(nc.vector.reciprocal(c1(RS + k), c1(GM + k)))
                link(ts(c1(RS + k), c1(RS + k), XQ, None, ALU.mult))

            def quant(c, k, src):
                wait(dve, q_ready, 2 * (NCH * k + c - 1))
                for px in (slice(0, HALF + W), slice(HALF + W, HW)):
                    ts(qf[:, c % 2, px], src[:, c, px], c1(RS + k), MAGIC, ALU.mult, ALU.add).then_inc(q_v, 1)

            link(tt(c1(PQ, w=2), c1(SW, w=2), bn[:, BSC, BNQ1:BNQ2 + 1], ALU.mult))
            ts(c1(PQ, w=2), c1(PQ, w=2), 1.0 / XQ, None, ALU.mult)
            step(0)
            quant(0, 0, y0)
            quant(1, 0, y0)
            tt(c1(SIG), c1(GM), c1(PQ), ALU.mult).then_inc(scale_ready, 1)
            for c in range(2, NCH):
                quant(c, 0, y0)
            for k in range(2):
                link(ts(wcr[:, k, :], wcr[:, k, :], c1(IPW + k), F16_TOP, ALU.mult, ALU.mult))
                link(nc.vector.tensor_copy(wst[:, k, :], wcr[:, k, :]))
                up = slice(2 * C, P)
                tt(wst[up, k, :], wcr[up, k, :], wst[up, k, :], ALU.subtract).then_inc(wst_ready, 1)
            tt(c1(KK), mxa[:, MW2:MW2 + 1], mxa[:, MI2:MI2 + 1], ALU.mult)
            link(tt(c1(KK + 1), mxa[:, MC:MC + 1], mxa[:, MIC:MIC + 1], ALU.mult))
            link(ts(c1(KK, w=2), c1(KK, w=2), float(TAPS * C), None, ALU.mult))
            link(tt(c1(PC, w=2), c1(PWR, w=2), bn[:, BSC, BNC:BND + 1], ALU.mult))
            ts(c1(PC, w=2), c1(PC, w=2), 1.0 / F16_TOP, None, ALU.mult)
            link(tt(c1(AA), c1(GM), mxa[:, MH2:MH2 + 1], ALU.add))
            stt(c1(AA + 1), c1(AA), c1(KK + 1), mxa[:, MHC:MHC + 1], ALU.mult, ALU.add)
            nc.vector.tensor_copy(c1(KP), c1(KK))
            tt(c1(KP + 1), c1(KK), c1(KK + 1), ALU.mult)
            for c in range(NCH):
                for h in range(2):
                    dve.wait_ge(h1_ready, 2 * c + h + 1)
                    red(cm[:, 1, c, h:h + 1], h1[:, c, HALF * h:HALF * h + HALF], AX.X,
                        ALU.max).then_inc(cmax_done, 1)
            step(1)
            quant(0, 1, h1)
            link(stt(c1(BD, w=2), c1(KP, w=2), c1(GM + 1), c1(AA, w=2), ALU.mult, ALU.add))
            link(ts(c1(BD, w=2), c1(BD, w=2), 1e-30, 1.0 / F16_TOP, ALU.max, ALU.mult))
            link(ts(c1(BD, w=2).bitcast(I32), c1(BD, w=2).bitcast(I32), 0x7F800000, None, ALU.bitwise_and))
            link(nc.vector.reciprocal(c1(BD + 2, w=2), c1(BD, w=2)))
            ts(c1(CUTS), c1(BD + 3), CUT, None, ALU.mult)
            tt(c1(SIG + 3), c1(BD + 2), bn[:, BSH, BNQ2:BNQ2 + 1], ALU.mult)
            stt(c1(SIG + 1), c1(BD + 2), c1(GM + 1), c1(PQ + 1), ALU.mult, ALU.mult)
            tt(c1(SIG + 4, w=2), c1(BD, w=2), c1(PC, w=2), ALU.mult).then_inc(scale_ready, 1)
            quant(1, 1, h1)
            for c in range(2, NCH):
                quant(c, 1, h1)

            def stack(layer, c):
                dve.wait_ge(part_ready[layer], 2 * c + 2)
                wait(dve, lconv_done[layer], 2 * (c - 1))
                if layer == 1:
                    at = LTAIL.index(("c", c))
                    dve.wait_ge(keep_ready, at + 1)
                flat = "p h w -> p (h w)"
                for g, k in V_SHARE:
                    q = slice(C * g, C * g + C)
                    dst = kst[C * k:C * k + C, layer, c % 2, g].rearrange(flat)
                    src = part[q, layer, c % 2, k].rearrange(flat)
                    if layer == 0:
                        i = nc.vector.tensor_copy(dst, src)
                    else:
                        i = ts(dst, src, keep[q, at:at + 1], None, ALU.mult)
                i.then_inc(stack_v[layer], 1)
                if (layer, c) in V_DUP:
                    dve.wait_ge(stack_v[layer], c + 1)
                    dve.wait_ge(stack_a[layer], c + 1)
                    images = kst[:, layer, c % 2].rearrange("p g h w -> p (g h w)")
                    nc.vector.tensor_copy(images[2 * C:P], images[0:2 * C]).then_inc(v_dup, 1)

            def halves_l(layer, c):
                if layer == 1 and c == 0:
                    dve.wait_ge(pool_zeroed, 11)
                if c >= 2:
                    dve.wait_ge(stack_a[layer], c - 1)
                return (inner(part[:, layer, c % 2, k]) for k in range(2))

            for kind, c in TAIL:
                if kind == "q":
                    dve.wait_ge(q2_done, 2 * (c + 1))
                    dve.wait_ge(ys_ready, c + 1)
                    qb = QBANK[c % 2]
                    stt(img(t1[:, c % 2, :], 2), ps[:, qb:qb + 2, :HALF], c1(SIG + 1), img(y0[:, c, :], 2),
                        ALU.mult, ALU.add).then_inc(t1_ready, 1)
                    hi, lo = halves_l(0, c)
                    dve.wait_ge(t1_ready, c + 1)
                    ts(hi, img(t1[:, c % 2, :]), 0.0, None, ALU.max).then_inc(part_ready[0], 1)
                    dve.wait_ge(part_ready[0], 2 * c + 1)
                    stt(lo, img(t1[:, c % 2, :]), 0.0, hi, ALU.max, ALU.subtract).then_inc(part_ready[0], 1)
                    stack(0, c)
                elif kind == "c":
                    at = LTAIL.index((kind, c))
                    hi, lo = halves_l(1, c)
                    y = img(yb[:, at % 2, :])
                    for h in range(2):
                        rows = slice(HALF_ROWS * h, HALF_ROWS * h + HALF_ROWS)
                        dve.wait_ge(yb_ready, 2 * at + h + 1)
                        i = ts(hi[:, rows], y[:, rows], c1(BD + 3), None, ALU.mult, ALU.max,
                               accum_out=cm[:, 0, c, h:h + 1])
                    i.then_inc(part_ready[1], 1)
                    dve.wait_ge(part_ready[1], 2 * c + 1)
                    stt(lo, y, c1(BD + 3), hi, ALU.mult, ALU.subtract).then_inc(part_ready[1], 1)
                    ts(keep[:, at:at + 1], cm[:, 0, c, 0:1], cm[:, 0, c, 1:2], c1(CUTS), ALU.max,
                       ALU.is_ge).then_inc(keep_ready, 1)
                    stack(1, c)
                else:
                    at = LTAIL.index((kind, c))
                    m = keep[:, at:at + 1]
                    px = [slice(HALF * h, HALF * h + HALF) for h in range(2)]
                    for h in range(2):
                        dve.wait_ge(yb_ready, 2 * at + h + 1)
                        i = red(cm[:, 1, c, h:h + 1], yb[:, at % 2, px[h]], AX.X, ALU.max)
                    link(i)
                    ts(m, cm[:, 1, c, 0:1], cm[:, 1, c, 1:2], CUT, ALU.max, ALU.is_ge).then_inc(keep_ready, 1)
                    if c == NCH - 1:
                        dve.wait_ge(keep_ready, at + 1)
                        for h in range(2):
                            ts(om[:, c, px[h]], yb[:, at % 2, px[h]], m, None, ALU.mult).then_inc(last_ready, 1)


def kernel(**inputs):
    import numpy as np
    import concourse.bacc as bacc
    from concourse.bass_utils import run_bass_kernel_spmd

    a = {k: np.asarray(v) for k, v in inputs.items()}

    def blocks(v):
        return np.ascontiguousarray(v.reshape(NCH, G, C, HW).transpose(1, 2, 0, 3).reshape(P, NCH, HW))

    def taps_first(w):
        return np.ascontiguousarray(w.transpose(1, 2, 3, 0).reshape(w.shape[1], -1))

    def column(kind):
        names = {"g": ("L1_conv_bn%d_gamma", "gamma"), "b": ("L1_conv_bn%d_beta", "beta"),
                 "m": ("L1_conv_bn%d_mean", "run_mean"), "v": ("L1_conv_bn%d_var", "run_var")}[kind]
        cols = []
        for k in (1, 2):
            v = a[f"L0_conv_{kind}{k}"]
            cols += [v[:P], np.tile(v[P:], 2)]
        cols.append(np.tile(a[f"L0_conv_{kind}3"], G))
        cols += [np.tile(a[names[0] % k], G) for k in (1, 2)]
        cols += [np.tile(a[f"L{k}_conv_{names[1]}"], G) for k in (2, 3)]
        return cols

    params = np.stack([c for kind in "gbmv" for c in column(kind)]
                      + [np.tile(a[f"L{k}_conv_conv_b"], G) for k in (2, 3)], axis=1)
    w2 = taps_first(a["L0_conv_w2"])
    arrays = {
        "x_in": blocks(a["x"]), "params_in": np.ascontiguousarray(params),
        "w1_in": taps_first(a["L0_conv_w1"]), "w2a_in": w2[:P], "w2b_in": np.ascontiguousarray(w2[P:]),
        "w3_in": taps_first(a["L0_conv_w3"]), "wq1_in": taps_first(a["L1_conv_w1"]),
        "wq2_in": taps_first(a["L1_conv_w2"]), "wc_in": taps_first(a["L2_conv_conv_w"]),
        "wd_in": taps_first(a["L3_conv_conv_w"]),
    }
    nc = bacc.Bacc("TRN2", target_bir_lowering=False, num_devices=1)
    args = [nc.dram_tensor(n, v.shape, F32, kind="ExternalInput").ap() for n, v in arrays.items()]
    out = nc.dram_tensor("y_out", (P, NCH, HW), F32, kind="ExternalOutput").ap()
    conv_seq(nc, *args, out)
    r = run_bass_kernel_spmd(nc, [arrays], core_ids=[0])
    y = np.asarray(r.results[0]["y_out"])
    return np.ascontiguousarray(y.reshape(G, C, NCH, H, W).transpose(2, 0, 1, 3, 4).reshape(B, C, H, W))
```
